# Optimizing a Trainium2 kernel written in Bass

```python
import numpy as np
import jax
import jax.numpy as jnp

def _softmax(x, axis=-1):
    return jax.nn.softmax(x, axis=axis)

def _gelu(x):
    return jax.nn.gelu(x, approximate=True)

def _silu(x):
    return jax.nn.silu(x)

def _sigmoid(x):
    return jax.nn.sigmoid(x)

def _layernorm(x, axis=-1, eps=1e-05):
    m = jnp.mean(x, axis=axis, keepdims=True)
    v = jnp.var(x, axis=axis, keepdims=True)
    return (x - m) / jnp.sqrt(v + eps)

def _scatter_add(tgt, idx, src, axis=0):
    return tgt.at[idx].add(src)

def _segment_sum(src, seg, n):
    return jax.ops.segment_sum(src, seg, n)
kernel_name = 'mk_hybrid_d1_jaxref_r4_a5b6dc'

def setup_inputs(seed: int=0):
    np.random.seed(seed)
    _w = jnp.asarray

    def _L0_attn_a_setup():
        import jax, jax.numpy as jnp
        import numpy as np
        DIM = 256
        NUM_HEADS = 16
        HEAD_DIM = DIM // NUM_HEADS
        EPS = 1e-06

        def _apply_rope(q, k):
            B, N, H, D = q.shape
            half = D // 2
            freqs = 1.0 / 2500 ** (jnp.arange(0, half, dtype=jnp.float32) / half)
            t = jnp.arange(N, dtype=jnp.float32)
            freqs = jnp.outer(t, freqs)
            emb = jnp.concatenate([freqs, freqs], axis=-1)
            cos = jnp.cos(emb)[None, :, None, :]
            sin = jnp.sin(emb)[None, :, None, :]

            def rot(x):
                x1, x2 = (x[..., :half], x[..., half:])
                return jnp.concatenate([-x2, x1], axis=-1)
            return (q * cos + rot(q) * sin, k * cos + rot(k) * sin)

        def _rmsnorm(x, scale):
            var = jnp.mean(jnp.square(x.astype(jnp.float32)), axis=-1, keepdims=True)
            return (x * jax.lax.rsqrt(var + EPS) * scale).astype(x.dtype)
        key = jax.random.key(seed)
        ks = jax.random.split(key, 6)
        B, N = (4, 512)
        x = jax.random.normal(ks[0], (B, N, DIM), dtype=jnp.float32)
        lim_qkv = float(np.sqrt(6.0 / (DIM + 3 * DIM)))
        w_qkv = jax.random.uniform(ks[1], (DIM, 3 * DIM), jnp.float32, -lim_qkv, lim_qkv)
        q_scale = jnp.ones((HEAD_DIM,), jnp.float32)
        k_scale = jnp.ones((HEAD_DIM,), jnp.float32)
        lim_p = float(np.sqrt(6.0 / (DIM + DIM)))
        w_proj = jax.random.uniform(ks[2], (DIM, DIM), jnp.float32, -lim_p, lim_p)
        b_proj = jnp.zeros((DIM,), jnp.float32)
        return {'x': x, 'w_qkv': w_qkv, 'q_scale': q_scale, 'k_scale': k_scale, 'w_proj': w_proj, 'b_proj': b_proj}
    _L0_attn_a_in = _L0_attn_a_setup()

    def _L0_attn_b_setup():
        import jax, jax.numpy as jnp
        import numpy as np
        from jax import lax
        D_MODEL, D_INNER, D_STATE, DT_RANK, D_CONV = (256, 512, 16, 64, 4)
        B, L = (2, 256)

        def _depthwise_conv_same(x, k, b):
            kw = k.shape[0]
            y = lax.conv_general_dilated(x, k, window_strides=(1,), padding=[((kw - 1) // 2, kw // 2)], dimension_numbers=('NWC', 'WIO', 'NWC'), feature_group_count=x.shape[-1])
            return y + b

        def _selective_scan(u, delta, A, Bm, Cm, Dv):
            deltaA = jnp.exp(jnp.einsum('bld,dn->bldn', delta, A))
            deltaB_u = (delta * u)[..., None] * Bm[:, :, None, :]
            dA = jnp.transpose(deltaA, (1, 0, 2, 3))
            dBu = jnp.transpose(deltaB_u, (1, 0, 2, 3))
            Ct = jnp.transpose(Cm, (1, 0, 2))
            h0 = jnp.zeros((u.shape[0], u.shape[2], A.shape[1]), u.dtype)

            def step(h, t):
                dA_t, dBu_t, C_t = t
                h = dA_t * h + dBu_t
                return (h, jnp.einsum('bdn,bn->bd', h, C_t))
            _, ys = lax.scan(step, h0, (dA, dBu, Ct))
            y = jnp.transpose(ys, (1, 0, 2))
            return y + u * Dv
        key = jax.random.key(seed)
        ks = jax.random.split(key, 8)
        f32 = jnp.float32
        return {'inputs': jax.random.normal(ks[0], (B, L, D_MODEL), f32), 'W_in': jax.random.normal(ks[1], (D_MODEL, 2 * D_INNER), f32) / np.sqrt(D_MODEL), 'K_conv': jax.random.normal(ks[2], (D_CONV, 1, D_INNER), f32) / np.sqrt(D_CONV), 'b_conv': jnp.zeros((D_INNER,), f32), 'W_x': jax.random.normal(ks[3], (D_MODEL, DT_RANK + 2 * D_STATE), f32) / np.sqrt(D_MODEL), 'W_dt': jax.random.normal(ks[4], (DT_RANK, D_INNER), f32) / np.sqrt(DT_RANK), 'b_dt': jnp.zeros((D_INNER,), f32), 'A_log': 0.02 * jax.random.normal(ks[5], (D_INNER, D_STATE), f32), 'D': jnp.ones((D_INNER,), f32), 'W_out': jax.random.normal(ks[6], (D_INNER, D_MODEL), f32) / np.sqrt(D_INNER), 'b_out': jnp.zeros((D_MODEL,), f32)}
    _L0_attn_b_in = _L0_attn_b_setup()

    def _L0_ffn_setup():
        import jax, jax.numpy as jnp
        import numpy as np
        EPS = 1e-05

        def _quantize(W):
            gamma = jnp.mean(jnp.abs(W))
            return jnp.clip(jnp.round(W / (gamma + EPS)), -1.0, 1.0)
        key = jax.random.key(seed)
        k_x, k_w1, k_b1, k_w2, k_b2 = jax.random.split(key, 5)
        n_embd = 256
        d_ff = 4 * n_embd
        B, S = (4, 1024)
        bound1 = 1.0 / np.sqrt(n_embd)
        bound2 = 1.0 / np.sqrt(d_ff)
        x = jax.random.normal(k_x, (B, S, n_embd), dtype=jnp.float32)
        W1 = jax.random.uniform(k_w1, (d_ff, n_embd), jnp.float32, -bound1, bound1)
        b1 = jax.random.uniform(k_b1, (d_ff,), jnp.float32, -bound1, bound1)
        W2 = jax.random.uniform(k_w2, (n_embd, d_ff), jnp.float32, -bound2, bound2)
        b2 = jax.random.uniform(k_b2, (n_embd,), jnp.float32, -bound2, bound2)
        return {'x': x, 'W1': W1, 'b1': b1, 'W2': W2, 'b2': b2}
    _L0_ffn_in = _L0_ffn_setup()
    _d = {'L0_attn_a_x': _L0_attn_a_in['x'], 'L0_attn_a_w_qkv': _L0_attn_a_in['w_qkv'], 'L0_attn_a_q_scale': _L0_attn_a_in['q_scale'], 'L0_attn_a_k_scale': _L0_attn_a_in['k_scale'], 'L0_attn_a_w_proj': _L0_attn_a_in['w_proj'], 'L0_attn_a_b_proj': _L0_attn_a_in['b_proj'], 'L0_attn_b_W_in': _L0_attn_b_in['W_in'], 'L0_attn_b_K_conv': _L0_attn_b_in['K_conv'], 'L0_attn_b_b_conv': _L0_attn_b_in['b_conv'], 'L0_attn_b_W_x': _L0_attn_b_in['W_x'], 'L0_attn_b_W_dt': _L0_attn_b_in['W_dt'], 'L0_attn_b_b_dt': _L0_attn_b_in['b_dt'], 'L0_attn_b_A_log': _L0_attn_b_in['A_log'], 'L0_attn_b_D': _L0_attn_b_in['D'], 'L0_attn_b_W_out': _L0_attn_b_in['W_out'], 'L0_attn_b_b_out': _L0_attn_b_in['b_out'], 'L0_ffn_W1': _L0_ffn_in['W1'], 'L0_ffn_b1': _L0_ffn_in['b1'], 'L0_ffn_W2': _L0_ffn_in['W2'], 'L0_ffn_b2': _L0_ffn_in['b2']}
    _x0 = _d['L0_attn_a_x']
    _d['L0_attn_a_x'] = jax.random.normal(jax.random.fold_in(jax.random.key(seed), 1), (8, 512, 256), dtype=_x0.dtype)
    del _x0
    return _d

def reference(L0_attn_a_x, L0_attn_a_w_qkv, L0_attn_a_q_scale, L0_attn_a_k_scale, L0_attn_a_w_proj, L0_attn_a_b_proj, L0_attn_b_W_in, L0_attn_b_K_conv, L0_attn_b_b_conv, L0_attn_b_W_x, L0_attn_b_W_dt, L0_attn_b_b_dt, L0_attn_b_A_log, L0_attn_b_D, L0_attn_b_W_out, L0_attn_b_b_out, L0_ffn_W1, L0_ffn_b1, L0_ffn_W2, L0_ffn_b2):

    def _L0_attn_a_ref(x, w_qkv, q_scale, k_scale, w_proj, b_proj):
        import jax, jax.numpy as jnp
        import numpy as np
        DIM = 256
        NUM_HEADS = 16
        HEAD_DIM = DIM // NUM_HEADS
        EPS = 1e-06

        def _apply_rope(q, k):
            B, N, H, D = q.shape
            half = D // 2
            freqs = 1.0 / 2500 ** (jnp.arange(0, half, dtype=jnp.float32) / half)
            t = jnp.arange(N, dtype=jnp.float32)
            freqs = jnp.outer(t, freqs)
            emb = jnp.concatenate([freqs, freqs], axis=-1)
            cos = jnp.cos(emb)[None, :, None, :]
            sin = jnp.sin(emb)[None, :, None, :]

            def rot(x):
                x1, x2 = (x[..., :half], x[..., half:])
                return jnp.concatenate([-x2, x1], axis=-1)
            return (q * cos + rot(q) * sin, k * cos + rot(k) * sin)

        def _rmsnorm(x, scale):
            var = jnp.mean(jnp.square(x.astype(jnp.float32)), axis=-1, keepdims=True)
            return (x * jax.lax.rsqrt(var + EPS) * scale).astype(x.dtype)
        B, N, C = x.shape
        qkv = jnp.einsum('bnc,cd->bnd', x, w_qkv).reshape(B, N, 3, NUM_HEADS, HEAD_DIM)
        q, k, v = (qkv[:, :, 0], qkv[:, :, 1], qkv[:, :, 2])
        q = _rmsnorm(q, q_scale)
        k = _rmsnorm(k, k_scale)
        q, k = _apply_rope(q, k)
        q = q.astype(jnp.float32) * HEAD_DIM ** (-0.5)
        k = k.astype(jnp.float32)
        v = v.astype(jnp.float32)
        logits = jnp.einsum('bqhd,bkhd->bhqk', q, k)
        attn = jax.nn.softmax(logits, axis=-1)
        out = jnp.einsum('bhqk,bkhd->bqhd', attn, v).reshape(B, N, C)
        return jnp.einsum('bnc,cd->bnd', out, w_proj) + b_proj

    def _L0_attn_b_ref(inputs, W_in, K_conv, b_conv, W_x, W_dt, b_dt, A_log, D, W_out, b_out):
        import jax, jax.numpy as jnp
        import numpy as np
        from jax import lax
        D_MODEL, D_INNER, D_STATE, DT_RANK, D_CONV = (256, 512, 16, 64, 4)
        B, L = (2, 256)

        def _depthwise_conv_same(x, k, b):
            kw = k.shape[0]
            y = lax.conv_general_dilated(x, k, window_strides=(1,), padding=[((kw - 1) // 2, kw // 2)], dimension_numbers=('NWC', 'WIO', 'NWC'), feature_group_count=x.shape[-1])
            return y + b

        def _selective_scan(u, delta, A, Bm, Cm, Dv):
            deltaA = jnp.exp(jnp.einsum('bld,dn->bldn', delta, A))
            deltaB_u = (delta * u)[..., None] * Bm[:, :, None, :]
            dA = jnp.transpose(deltaA, (1, 0, 2, 3))
            dBu = jnp.transpose(deltaB_u, (1, 0, 2, 3))
            Ct = jnp.transpose(Cm, (1, 0, 2))
            h0 = jnp.zeros((u.shape[0], u.shape[2], A.shape[1]), u.dtype)

            def step(h, t):
                dA_t, dBu_t, C_t = t
                h = dA_t * h + dBu_t
                return (h, jnp.einsum('bdn,bn->bd', h, C_t))
            _, ys = lax.scan(step, h0, (dA, dBu, Ct))
            y = jnp.transpose(ys, (1, 0, 2))
            return y + u * Dv
        x_and_res = inputs @ W_in
        x, res = jnp.split(x_and_res, 2, axis=-1)
        x = jax.nn.silu(_depthwise_conv_same(x, K_conv, b_conv))
        A = -jnp.exp(A_log)
        x_dbl = inputs @ W_x
        delta, Bm, Cm = jnp.split(x_dbl, [DT_RANK, DT_RANK + D_STATE], axis=-1)
        delta = jax.nn.softplus(delta @ W_dt + b_dt)
        y = _selective_scan(x, delta, A, Bm, Cm, D)
        y = y * jax.nn.silu(res)
        return y @ W_out + b_out

    def _L0_ffn_ref(x, W1, b1, W2, b2):
        import jax, jax.numpy as jnp
        import numpy as np
        EPS = 1e-05

        def _quantize(W):
            gamma = jnp.mean(jnp.abs(W))
            return jnp.clip(jnp.round(W / (gamma + EPS)), -1.0, 1.0)
        Wq1 = _quantize(W1)
        Wq2 = _quantize(W2)
        h = jax.nn.relu(jnp.einsum('bsd,fd->bsf', x, Wq1) + b1)
        out = jnp.einsum('bsf,df->bsd', h, Wq2) + b2
        return out
    x = L0_attn_a_x
    x = x + _L0_attn_a_ref(_layernorm(x, axis=-1), L0_attn_a_w_qkv, L0_attn_a_q_scale, L0_attn_a_k_scale, L0_attn_a_w_proj, L0_attn_a_b_proj)
    x = x + _L0_ffn_ref(_layernorm(x, axis=-1), L0_ffn_W1, L0_ffn_b1, L0_ffn_W2, L0_ffn_b2)
    x = x + _L0_attn_b_ref(_layernorm(x, axis=-1), L0_attn_b_W_in, L0_attn_b_K_conv, L0_attn_b_b_conv, L0_attn_b_W_x, L0_attn_b_W_dt, L0_attn_b_b_dt, L0_attn_b_A_log, L0_attn_b_D, L0_attn_b_W_out, L0_attn_b_b_out)
    x = x + _L0_ffn_ref(_layernorm(x, axis=-1), L0_ffn_W1, L0_ffn_b1, L0_ffn_W2, L0_ffn_b2)
    return x

_drawn_inputs = setup_inputs


def setup_inputs(seed=0):
    import zlib

    import numpy as np

    out = dict(_drawn_inputs(seed))
    spreads = {'L0_attn_a_q_scale': (1.0, 0.2),
     'L0_attn_a_k_scale': (1.0, 0.2),
     'L0_attn_a_b_proj': (0.0, 0.1),
     'L0_attn_b_b_conv': (0.0, 0.1),
     'L0_attn_b_b_dt': (0.0, 0.1),
     'L0_attn_b_D': (1.0, 0.2),
     'L0_attn_b_b_out': (0.0, 0.1)}
    factors = {}
    for name, (base, spread) in spreads.items():
        noise = np.random.default_rng([zlib.crc32(name.encode()), seed]).standard_normal(out[name].shape)
        drawn = base * np.exp(spread * noise) if base else spread * noise
        out[name] = jnp.asarray(drawn.astype(out[name].dtype))
    for name, factor in factors.items():
        out[name] = (out[name] * factor).astype(out[name].dtype)
    return out
```

```python
import numpy as np
import concourse.bass as bass
from concourse import mybir
from contextlib import ExitStack

FP32 = mybir.dt.float32
FP16 = mybir.dt.float16
ALU = mybir.AluOpType
ACT = mybir.ActivationFunctionType
AX = mybir.AxisListType

BATCH, SEQ, DIM = 8, 512, 256
P = 128
TT = SEQ // P
KC = DIM // P
HEADS = 16
HD = DIM // HEADS
HALF = HD // 2
ROWS = 64
D_INNER = 512
DT = D_INNER // P
NS = 16
RANK = 64
XD = RANK + 2 * NS
FF = 1024
FC = FF // P
CONV = 4
LN_EPS = 1e-5
RMS_EPS = 1e-6
EXP_LN = "natural_log_exp_and_others"
Q_EPS = 1e-5
SHIFT = 3 * HD
GROUP = 4
PSLOTS = 8
HSLOTS = 3
LN_BOUND = 256.0
MAX_LOGIT_UNSHIFTED = 60.0


def hybrid_block(nc, t, out, cos_t, sin_t, bt_scratch):
    x_d, y_d = t["L0_attn_a_x"], out

    with ExitStack() as ctx:
        def sb(name, shape, dt=FP32):
            return ctx.enter_context(nc.sbuf_tensor(name, shape, dt))

        def sem(name):
            return ctx.enter_context(nc.semaphore(name))

        wqkv_hi = sb("wqkv_hi", [P, KC, 3 * DIM], FP16)
        wqkv_lo = sb("wqkv_lo", [P, KC, 3 * DIM], FP16)
        win_hi = sb("win_hi", [P, KC, 2 * D_INNER], FP16)
        win_lo = sb("win_lo", [P, KC, 2 * D_INNER], FP16)
        wx_hi = sb("wx_hi", [P, KC, XD], FP16)
        wx_lo = sb("wx_lo", [P, KC, XD], FP16)
        wdt = sb("wdt", [RANK, D_INNER])
        wproj = sb("wproj", [P, KC, DIM])
        wout = sb("wout", [P, DT, DIM])
        w1t = sb("w1t", [P, KC, FF], FP16)
        w2t = sb("w2t", [P, FC, DIM], FP16)
        bproj = sb("bproj", [P, DIM])
        bout = sb("bout", [P, DIM])
        b2 = sb("b2", [P, DIM])
        b1 = sb("b1", [P, FC])
        bdt = sb("bdt", [P, DT])
        bconv = sb("bconv", [P, DT])
        dskip = sb("dskip", [P, DT])
        kconv = sb("kconv", [P, DT, CONV])
        aneg = sb("aneg", [P, DT, NS])
        ropec = sb("ropec", [P, 2, TT, HD])
        ropes = sb("ropes", [P, 2, TT, HD])
        identf = sb("identf", [P, P])
        identh = sb("identh", [P, P], FP16)
        sc = sb("sc", [P, 32])
        big_logits = sb("big_logits", [P, 1], mybir.dt.uint32)
        rowmax = sb("rowmax", [P, TT * HEADS])
        ones8 = sb("ones8", [8, P])
        red = sb("red", [8, 2])
        reddiag = sb("reddiag", [8, 16])
        xa = sb("xa", [P, TT, DIM])
        xb = sb("xb", [P, TT, DIM])
        yo = sb("yo", [P, TT, DIM])
        xn = sb("xn", [P, TT, DIM])
        bnst = sb("bnst", [P, TT, 6])
        mv = sb("mv", [P, TT, 2])
        lnv = sb("lnv", [P, TT])
        rstd = sb("rstd", [P, TT])
        xt_hi = sb("xt_hi", [P, KC, SEQ], FP16)
        xt_lo = sb("xt_lo", [P, KC, SEQ], FP16)
        qt = sb("qt", [P, HEADS // 2, SEQ], FP16)
        kt = sb("kt", [P, HEADS // 2, SEQ], FP16)
        vaug = sb("vaug", [P, TT, HEADS, 2 * HD])
        ot = xn[:, 0:2, :].rearrange("p a n -> p (a n)")
        rden = sb("rden", [P, TT, GROUP])
        on = sb("on", [P, TT, DIM])
        msq = sb("msq", [P, 2 * TT * HEADS])
        rms = sb("rms", [P, 2 * TT * HEADS])
        delta = sb("delta", [P, DT, SEQ])
        u = sb("u", [P, DT, SEQ])
        du = sb("du", [P, DT, SEQ])
        sres = sb("sres", [P, DT, SEQ])
        xdbl = sb("xdbl", [XD, SEQ])
        ctok = sb("ctok", [P, TT, NS])
        acc = sb("acc", [P, TT, D_INNER])
        decay = sb("decay", [P, 2, DT, SEQ])
        hst = sb("hst", [P, HSLOTS, DT, SEQ])
        bbc = sb("bbc", [P, 2, SEQ])
        ybuf = delta
        convtmp = hst[:, 1, :, :]
        xpad = acc[:, :, :].rearrange("p (i a) n -> p i (a n)", i=2)[:, :, 0:SEQ + CONV - 1]
        arena = sb("arena", [P, PSLOTS * 2 * SEQ])
        prob = arena[:, :].rearrange("p (s k q) -> p s k q", s=PSLOTS, k=2)
        W = TT * SEQ
        qk = arena[:, 0:W].rearrange("p (a n) -> p a n", a=2 * TT)
        sq = arena[:, W:2 * W]
        qn = arena[:, 2 * W:3 * W]
        rot = arena[:, 3 * W:4 * W]
        qka = arena[:, 0:2 * W].bitcast(FP16).rearrange("p (a h r) -> p a h r", h=TT * HEADS, r=ROWS)
        hid = arena[:, 0:W].rearrange("p (s n) -> p s n", s=4)
        h_hi = arena[:, W:2 * W].bitcast(FP16).rearrange("p (f n) -> p f n", f=FC)
        h_lo = arena[:, 2 * W:3 * W].bitcast(FP16).rearrange("p (f n) -> p f n", f=FC)
        oc = arena[:, 3 * W:3 * W + KC * SEQ].rearrange("p (c n) -> p c n", c=KC)
        ldq = arena[:, 0:KC * 3 * DIM].rearrange("p (c n) -> p c n", c=KC)
        ldi = arena[:, 1536:1536 + KC * 2 * D_INNER].rearrange("p (c n) -> p c n", c=KC)
        ldx = arena[:, 3584:3584 + KC * XD].rearrange("p (c n) -> p c n", c=KC)
        ldw1 = sres[:, :, :].rearrange("p a n -> p (a n)").rearrange("p (f n) -> p f n", f=FC)
        ldw2 = u[:, :, :].rearrange("p a n -> p (a n)").rearrange("p (c n) -> p c n", c=KC)
        accf = acc[:, :, :].rearrange("p a n -> p (a n)")
        tern1 = accf[:, 0:1024].bitcast(FP16).rearrange("p (f n) -> p f n", f=FC)
        tern2 = accf[:, 1024:2048].bitcast(FP16).rearrange("p (c n) -> p c n", c=KC)
        stmp = du[:, :, :].rearrange("p a n -> p (a n)")
        qsc = sb("qsc", [P, 2, 2, HD])

        ps = ctx.enter_context(nc.psum_tensor("ps", [P, 8, SEQ], FP32))
        psh = [ps[:, i, :].bitcast(FP16) for i in range(8)]

        (A_QKV, A_IN, A_X, G1, G2, MQ, MK, MB, I_QKV, I_IN, I_X, TH1, TH2, NTH1, NTH2, LOGIT, S_H,
         INV_S, EPS_LN, EPS_RMS, IQ, IK, TMP, R0, R1) = range(25)

        def col(i, n=1):
            return sc[:, i:i + n]

        UNITS = 2 * HEADS
        NG = HEADS // GROUP
        PVS = UNITS // GROUP

        def unit(i):
            g, pair, j = i // (2 * GROUP), i // GROUP % 2, i % GROUP
            return g * GROUP + j, 2 * pair

        QK_BANK = [6, 7, 0, 1, 2, 3, 6, 7]
        X_BANK, DT_BANK, RES_BANK = [1, 2, 3, 4], [1, 2, 3, 4], [5, 6, 7, 0]
        n_loads = [0]

        def stand_alone(eng):
            eng.sem_inc(s["waited"], 1)

        def qk_evac(j):
            dst = (qt, kt)[j // 4]
            return dst[:, (j % 4) * 2:(j % 4) * 2 + 2, :], psh[QK_BANK[j]].rearrange("p (a n) -> p a n", a=2)

        def heads_view(flat):
            return flat.rearrange("p (a h d) -> p a h d", a=2 * TT, d=HD)

        names = """ld_w ld_x setup_v setup_p setup_a setup_r setup_t setup_tev setup_ev
                   stats mv lnv rstd xn xt hi lo biased
                   qkv qkev vev msq_sq msq_red msq_ln msq_rs qn rot_s ropea roped qhi qlo qktp qkt
                   score prob pv oev otp qkta qktv rden on
                   decay dbu scan htp accd bload0 bload1 bstore
                   ytp yskip y wo woev
                   up hid hhi hlo down fout
                   ontp ocev proj pjev
                   xdp xdev ctp cev dtp zc ez lz delta xin xpad conv1 conv uu res du sres_ store waited guard_s guard_m guard_h guard_w guard_t guard_c
                   """.split()
        s = {n: sem("s_" + n) for n in names}

        block = ctx.enter_context(nc.Block())

        LAST = BATCH

        def iterations(eng, body):
            body(0, True, False)
            with eng.Fori(1, LAST) as b:
                body(b, True, True)
            body(LAST, False, True)

        def ln_before(kind, b):
            if isinstance(b, int) and b == 0 and kind == "attn":
                return 0
            if isinstance(b, int) and b == BATCH:
                return b * 4 - 1
            return b * 4 + {"attn": -1, "ffn2": 0, "ffn1": 1, "scan": 2}[kind]

        def ffn_before(kind, b):
            if isinstance(b, int) and b == 0:
                return 0
            return b * 2 - 1 + (1 if kind == "ffn1" else 0)

        @block.sync
        def _(sp):
            first = [
                (ldq, t["L0_attn_a_w_qkv"].rearrange("(c p) n -> p c n", p=P)),
                (ldi, t["L0_attn_b_W_in"].rearrange("(c p) n -> p c n", p=P)),
                (ldx, t["L0_attn_b_W_x"].rearrange("(c p) n -> p c n", p=P)),
                (ldw1, t["L0_ffn_W1"].rearrange("(f p) n -> p f n", p=P)),
                (ldw2, t["L0_ffn_W2"].rearrange("(c p) n -> p c n", p=P)),
                (wdt[:, :], t["L0_attn_b_W_dt"]),
                (wproj[:, :, :], t["L0_attn_a_w_proj"].rearrange("(c p) n -> p c n", p=P)),
                (wout[:, :, :], t["L0_attn_b_W_out"].rearrange("(c p) n -> p c n", p=P)),
                (bproj[:, :], t["L0_attn_a_b_proj"].partition_broadcast(P)),
                (bout[:, :], t["L0_attn_b_b_out"].partition_broadcast(P)),
                (b2[:, :], t["L0_ffn_b2"].partition_broadcast(P)),
                (qsc[:, 0, 0, :], t["L0_attn_a_q_scale"].partition_broadcast(P)),
                (qsc[:, 1, 0, :], t["L0_attn_a_k_scale"].partition_broadcast(P)),
                (ropec[:, 0, :, :], cos_t.rearrange("(a p) n -> p a n", p=P)),
                (ropec[:, 1, :, :], cos_t.rearrange("(a p) n -> p a n", p=P)),
                (ropes[:, 0, :, :], sin_t.rearrange("(a p) n -> p a n", p=P)),
                (ropes[:, 1, :, :], sin_t.rearrange("(a p) n -> p a n", p=P)),
                (aneg[:, :, :], t["L0_attn_b_A_log"].rearrange("(c p) n -> p c n", p=P)),
            ]
            for a in range(2):
                name = "L0_attn_a_q_scale" if a == 0 else "L0_attn_a_k_scale"
                for half in range(2):
                    first.append((qsc[:, a, 1, half * HALF:(half + 1) * HALF],
                                  t[name][(1 - half) * HALF:(2 - half) * HALF].partition_broadcast(P)))
            with nc.allow_non_contiguous_dma(reason="small vectors laid over partitions, once"):
                slow = [
                    (b1[:, :], t["L0_ffn_b1"].rearrange("(f p) -> p f", p=P)),
                    (bdt[:, :], t["L0_attn_b_b_dt"].rearrange("(f p) -> p f", p=P)),
                    (bconv[:, :], t["L0_attn_b_b_conv"].rearrange("(f p) -> p f", p=P)),
                    (dskip[:, :], t["L0_attn_b_D"].rearrange("(f p) -> p f", p=P)),
                ] + [(kconv[:, :, j], t["L0_attn_b_K_conv"][j, 0, :].rearrange("(f p) -> p f", p=P))
                     for j in range(CONV)]
                for dst, src in first + slow:
                    sp.dma_start(dst, src).then_inc(s["ld_w"], 16)
            n_loads[0] = len(first + slow)

            def load_b_row(m, n):
                if n >= 2:
                    sp.wait_ge(s["dbu"], m * NS + n - 1)
                    stand_alone(sp)
                sp.dma_start(bbc[:, n % 2, :], bt_scratch[n, :].partition_broadcast(P)).then_inc(s[("bload0", "bload1")[n % 2]], 16)

            def body(b, has_a, has_m):
                if has_a:
                    if not (isinstance(b, int) and b == 0):
                        sp.wait_ge(s["fout"], (b * 2 - 1) * TT)
                        stand_alone(sp)
                    sp.dma_start(xa[:, :, :], x_d[b].rearrange("(a p) n -> p a n", p=P)).then_inc(s["ld_x"], 16)
                if has_m:
                    sp.wait_ge(s["bstore"], b * 16)
                    stand_alone(sp)
                    for n in range(NS):
                        load_b_row(b - 1, n)
                    sp.wait_ge(s["fout"], (b * 2) * TT)
                    stand_alone(sp)
                    sp.dma_start(y_d[b - 1].rearrange("(a p) n -> p a n", p=P), yo[:, :, :]).then_inc(s["store"], 16)
                if has_a:
                    sp.wait_ge(s["xdev"], b + 1)
                    stand_alone(sp)
                    if has_m:
                        sp.wait_ge(s["dbu"], b * NS)
                    sp.dma_start(bt_scratch[:, :], xdbl[RANK:RANK + NS, :]).then_inc(s["bstore"], 16)

            iterations(sp, body)
            sp.wait_ge(s["store"], 16 * (BATCH + 1))

        @block.gpsimd
        def _(pool):
            nc.gpsimd.memset(identf[:, :], 0.0).then_inc(s["setup_p"], 1)
            nc.gpsimd.memset(identh[:, :], 0.0).then_inc(s["setup_p"], 1)
            pool.wait_ge(s["setup_p"], 2)
            for m in (identf, identh):
                nc.gpsimd.affine_select(out=m[:, :], in_=m[:, :], compare_op=ALU.not_equal, fill=1.0,
                                        base=0, pattern=[[-1, P]], channel_multiplier=1).then_inc(s["setup_p"], 1)
            nc.gpsimd.memset(vaug[:, :, :, HD:2 * HD], 1.0).then_inc(s["setup_p"], 1)
            nc.gpsimd.memset(ones8[:, :], 1.0).then_inc(s["setup_p"], 1)
            nc.gpsimd.memset(decay[:, :, :, 0:1], 0.0).then_inc(s["setup_p"], 1)
            nc.gpsimd.memset(yo[:, 0, 0:1], 0.0).then_inc(s["store"], 16)

            def add_bias(dst, bias, after_ln):
                pool.wait_ge(s["xn"], after_ln + 1)
                nc.gpsimd.tensor_tensor(dst[:, :, :], dst[:, :, :],
                                        bias[:, :].unsqueeze(1).to_broadcast([P, TT, DIM]),
                                        ALU.add).then_inc(s["biased"], 1)

            def hidden_cast(kind, b):
                g = ffn_before(kind, b)
                for f in range(FC):
                    pool.wait_ge(s["hid"], g * FC + f + 1)
                    stand_alone(pool)
                    nc.gpsimd.tensor_copy(h_hi[:, f, :], hid[:, f % 4, :]).then_inc(s["hhi"], 1)

            def body(b, has_a, has_m):
                if has_a:
                    add_bias(xa, bproj, ln_before("attn", b))
                    pool.wait_ge(s["msq_rs"], b + 1)
                    nc.gpsimd.tensor_tensor(
                        qn.rearrange("p (a d) -> p a d", d=HD),
                        qk.rearrange("p a (h d) -> p (a h) d", d=HD),
                        rms[:, :].unsqueeze(2).to_broadcast([P, 2 * TT * HEADS, HD]), ALU.mult).then_inc(s["qn"], 1)
                    pool.wait_ge(s["qn"], b + 1)
                    q4 = qn.rearrange("p (a h d) -> p a h d", a=2 * TT, d=HD)
                    r4 = rot.rearrange("p (a h d) -> p a h d", a=2 * TT, d=HD)
                    s3 = ropes[:, :, :, :].rearrange("p a b d -> p (a b) d")
                    for half in range(2):
                        lo_, hi_ = half * HALF, (half + 1) * HALF
                        so = (1 - half) * HALF
                        nc.gpsimd.tensor_tensor(
                            r4[:, :, :, lo_:hi_], q4[:, :, :, so:so + HALF],
                            s3[:, :, lo_:hi_].unsqueeze(2).to_broadcast([P, 2 * TT, HEADS, HALF]),
                            ALU.mult).then_inc(s["rot_s"], 1)
                if has_m:
                    pool.wait_ge(s["du"], b * DT)
                    for n in range(NS):
                        pool.wait_ge(s[("bload0", "bload1")[n % 2]], ((b - 1) * (NS // 2) + n // 2 + 1) * 16)
                        if n >= HSLOTS:
                            pool.wait_ge(s["htp"], ((b - 1) * NS + n - HSLOTS + 1) * TT)
                        nc.gpsimd.tensor_tensor(
                            hst[:, n % HSLOTS, :, :], du[:, :, :],
                            bbc[:, n % 2, :].unsqueeze(1).to_broadcast([P, DT, SEQ]), ALU.mult).then_inc(s["dbu"], 1)
                    add_bias(xb, b2, ln_before("ffn2", b))
                    hidden_cast("ffn2", b)
                if has_a:
                    add_bias(xa, b2, ln_before("ffn1", b))
                    hidden_cast("ffn1", b)
                    add_bias(xb, bout, ln_before("scan", b))
                    for d in range(DT):
                        pool.wait_ge(s["delta"], b * DT + d + 1)
                        pool.wait_ge(s["uu"], b * DT + d + 1)
                        nc.gpsimd.tensor_tensor(du[:, d, :], delta[:, d, :], u[:, d, :], ALU.mult).then_inc(s["du"], 1)

            iterations(pool, body)

        def bias_before(kind, b):
            return ln_before(kind, b)

        @block.scalar
        def _(act):
            nc.scalar.preload_act_table_set(EXP_LN)
            act.wait_ge(s["ld_w"], 16 * n_loads[0])
            nc.scalar.activation(aneg[:, :, :], aneg[:, :, :], ACT.Exp).then_inc(s["setup_a"], 1)
            act.wait_ge(s["setup_v"], 3)

            def layernorm(kind, b):
                i = ln_before(kind, b)
                act.wait_ge(s["mv"], i + 1)
                nc.scalar.activation(lnv[:, :], mv[:, :, 1], ACT.Ln, bias=col(EPS_LN)).then_inc(s["lnv"], 1)
                act.wait_ge(s["lnv"], i + 1)
                nc.scalar.activation(rstd[:, :], lnv[:, :], ACT.Exp, scale=-0.5).then_inc(s["rstd"], 1)
                act.wait_ge(s["xt"], i + 1)
                nc.scalar.activation(xt_hi[:, :, :], ps[:, 6:8, :], ACT.Copy).then_inc(s["hi"], 1)

            def ffn(kind, b):
                g = ffn_before(kind, b)
                for f in range(FC):
                    act.wait_ge(s["up"], g * FC + f + 1)
                    if f >= 4:
                        act.wait_ge(s["hlo"], g * FC + f - 3)
                    nc.scalar.activation(hid[:, f % 4, :], ps[:, f % 4, :], ACT.Relu,
                                         bias=b1[:, f:f + 1], scale=col(S_H)).then_inc(s["hid"], 1)

            def body(b, has_a, has_m):
                if has_a:
                    layernorm("attn", b)
                    for tt in range(TT):
                        act.wait_ge(s["qkv"], b * TT + tt + 1)
                        pq = ps[:, tt, :].rearrange("p (a n) -> p a n", a=2)
                        q4 = qk.rearrange("p (a b) n -> p a b n", a=2)
                        s4 = sq.rearrange("p (a b n) -> p a b n", a=2, b=TT)
                        nc.scalar.activation(q4[:, :, tt, :], pq, ACT.Copy, scale=col(A_QKV)).then_inc(s["qkev"], 1)
                        nc.scalar.activation(s4[:, :, tt, :], pq, ACT.Square, scale=col(A_QKV)).then_inc(s["msq_sq"], 1)
                    act.wait_ge(s["msq_red"], b + 1)
                    nc.scalar.activation(msq[:, :], msq[:, :], ACT.Ln, bias=col(EPS_RMS), scale=1.0 / HD).then_inc(s["msq_ln"], 1)
                    act.wait_ge(s["msq_ln"], b + 1)
                    nc.scalar.activation(rms[:, :], msq[:, :], ACT.Exp, scale=-0.5).then_inc(s["msq_rs"], 1)
                    act.wait_ge(s["roped"], b + 1)
                    for a in range(2):
                        step = 2 - a
                        src = rot[:, a * TT * DIM:(a + 1) * TT * DIM].rearrange("p (h d) -> p h d", d=HD)
                        for c in range(2):
                            o = c * step * HD
                            nc.scalar.activation(qka[:, a, :, o:o + HD], src, ACT.Copy).then_inc(s["qhi"], 1)
                    for j in range(0, 8, 2):
                        act.wait_ge(s["qktp"], b * 8 + j + 1)
                        nc.scalar.activation(*qk_evac(j), ACT.Copy).then_inc(s["qkta"], 1)
                def decays(n):
                    m = b - 1
                    if n == 0:
                        act.wait_ge(s["delta"], b * DT)
                    if n >= 2:
                        act.wait_ge(s["scan"], m * NS + n - 1)
                    for d in range(DT):
                        ins = nc.scalar.activation(decay[:, n % 2, d, 1:SEQ], delta[:, d, 1:SEQ], ACT.Exp,
                                                   scale=aneg[:, d, n:n + 1])
                    ins.then_inc(s["decay"], 1)

                def numerators(i):
                    act.wait_ge(s["score"], b * UNITS + i + 1)
                    if i >= PSLOTS:
                        act.wait_ge(s["pv"], b * PVS + (i - PSLOTS) // GROUP + 1)
                    bank = 2 * (i % 2)
                    nc.scalar.activation(prob[:, i % PSLOTS, :, :], ps[:, bank:bank + 2, :], ACT.Exp,
                                         scale=col(LOGIT)).then_inc(s["prob"], 1)

                if has_m:
                    decays(0)
                for n in range(NS):
                    if has_m and n + 1 < NS:
                        decays(n + 1)
                    if has_a:
                        numerators(2 * n)
                        numerators(2 * n + 1)
                if has_m:
                    layernorm("ffn2", b)
                    if has_a:
                        act.wait_ge(s["pv"], (b + 1) * PVS)
                    ffn("ffn2", b)
                if has_a:
                    act.wait_ge(s["ontp"], b + 1)
                    if not has_m:
                        act.wait_ge(s["pv"], (b + 1) * PVS)
                    nc.scalar.activation(oc, ps[:, 0:2, :], ACT.Copy).then_inc(s["ocev"], 1)
                    layernorm("ffn1", b)
                    ffn("ffn1", b)
                    layernorm("scan", b)
                    act.wait_ge(s["xdp"], b + 1)
                    if has_m:
                        act.wait_ge(s["bstore"], 16 * b)
                    nc.scalar.activation(xdbl[:, :], ps[0:XD, 0, :], ACT.Copy, scale=sc[0:XD, A_X:A_X + 1]).then_inc(s["xdev"], 1)
                    for d in range(DT):
                        act.wait_ge(s["zc"], b * DT + d + 1)
                        nc.scalar.activation(hst[:, 1, d, :], hst[:, 1, d, :], ACT.Exp).then_inc(s["ez"], 1)
                    for d in range(DT):
                        act.wait_ge(s["ez"], b * DT + d + 1)
                        nc.scalar.activation(hst[:, 1, d, :], hst[:, 1, d, :], ACT.Ln, bias=1.0).then_inc(s["lz"], 1)
                    for d in range(DT):
                        act.wait_ge(s["conv"], b * DT + d + 1)
                        nc.scalar.activation(u[:, d, :], hst[:, 0, d, :], ACT.Silu, bias=bconv[:, d:d + 1]).then_inc(s["uu"], 1)
                    for d in range(DT):
                        act.wait_ge(s["res"], b * DT + d + 1)
                        nc.scalar.activation(sres[:, d, :], ps[:, RES_BANK[d], :], ACT.Silu, scale=col(A_IN)).then_inc(s["sres_"], 1)
                    nc.scalar.preload_act_table_set(EXP_LN)

            iterations(act, body)

        @block.vector
        def _(dve):
            v = nc.vector
            dve.wait_ge(s["ld_w"], 16 * n_loads[0])
            dve.wait_ge(s["setup_p"], 7)
            k = [0]

            def link(ins):
                k[0] += 1
                ins.then_inc(s["setup_ev"], 1)
                dve.wait_ge(s["setup_ev"], k[0])

            for i, src, op in ((A_QKV, ldq, ALU.max), (A_IN, ldi, ALU.max), (A_X, ldx, ALU.max),
                               (G1, ldw1, ALU.add), (G2, ldw2, ALU.add)):
                v.tensor_reduce(col(i), src, AX.XY, op, apply_absolute_value=True)
            v.tensor_reduce(col(MQ), qsc[:, 0, 0, :], AX.X, ALU.max, apply_absolute_value=True)
            v.tensor_reduce(col(MK), qsc[:, 1, 0, :], AX.X, ALU.max, apply_absolute_value=True)
            v.memset(col(EPS_LN), LN_EPS)
            v.memset(col(EPS_RMS), RMS_EPS)
            v.tensor_reduce(col(MB), b1[:, :], AX.X, ALU.max, apply_absolute_value=True).then_inc(s["setup_v"], 1)
            dve.wait_ge(s["setup_p"], 4)
            dve.wait_ge(s["setup_r"], 1)
            link(v.tensor_reduce(red[:, 0:1], ps[0:8, 0, 0:P], AX.X, ALU.max))
            link(v.tensor_reduce(red[:, 1:2], ps[0:8, 0, 0:P], AX.X, ALU.add))
            link(v.tensor_scalar(reddiag[:, 0:8], identf[0:8, 0:8], red[:, 0:1], None, ALU.mult))
            v.tensor_scalar(reddiag[:, 8:16], identf[0:8, 0:8], red[:, 1:2], None, ALU.mult).then_inc(s["setup_v"], 1)
            dve.wait_ge(s["setup_r"], 2)
            link(v.tensor_copy(col(0, 3), ps[:, 1, 0:3]))
            link(v.tensor_copy(col(G1, 2), ps[:, 1, 8 + G1:8 + G1 + 2]))
            link(v.tensor_copy(col(MB), ps[:, 1, MB:MB + 1]))
            link(v.tensor_scalar(col(A_QKV, 3), col(A_QKV, 3), 1e-30, None, ALU.max))
            link(v.tensor_scalar(col(MQ, 2), col(MQ, 2), 1e-30, None, ALU.max))
            link(v.reciprocal(col(I_QKV, 3), col(A_QKV, 3)))
            link(v.reciprocal(col(IQ, 2), col(MQ, 2)))
            link(v.tensor_tensor(col(TMP), col(MQ), col(MK), ALU.mult))
            link(v.tensor_scalar(col(LOGIT), col(TMP), float(HD) ** -0.5, None, ALU.mult))
            link(v.tensor_scalar(big_logits[:, :], col(LOGIT), MAX_LOGIT_UNSHIFTED / HD, None, ALU.is_gt))
            link(v.tensor_scalar(col(TH1, 2), col(G1, 2), 1.0 / (FF * DIM), Q_EPS, ALU.mult, ALU.add))
            link(v.tensor_scalar(col(NTH1, 2), col(TH1, 2), -0.5, None, ALU.mult))
            link(v.tensor_scalar(col(TH1, 2), col(TH1, 2), 0.5, None, ALU.mult))
            link(v.tensor_scalar(col(INV_S), col(MB), 1.0 / LN_BOUND, 1.0, ALU.mult, ALU.add))
            link(v.reciprocal(col(S_H), col(INV_S)))
            link(v.tensor_scalar(b1[:, :], b1[:, :], col(S_H), None, ALU.mult))
            for i, src, hi_, lo_ in ((I_QKV, ldq, wqkv_hi, wqkv_lo), (I_IN, ldi, win_hi, win_lo), (I_X, ldx, wx_hi, wx_lo)):
                n = src.shape[1] * src.shape[2]
                link(v.tensor_scalar(src, src, col(i), None, ALU.mult))
                link(v.tensor_copy(hi_[:, :, :], src))
                link(v.tensor_tensor(lo_[:, :, :], src, hi_[:, :, :], ALU.subtract))
            for thr, nthr, src, dst in ((TH1, NTH1, ldw1, tern1), (TH2, NTH2, ldw2, tern2)):
                tmp = stmp.rearrange("p (f n) -> p f n", f=src.shape[1])
                link(v.tensor_scalar(tmp, src, col(nthr), None, ALU.is_lt))
                link(v.scalar_tensor_tensor(dst, src, col(thr), tmp, ALU.is_gt, ALU.subtract))
            for a in range(2):
                for tab, w in ((ropec, 0), (ropes, 1)):
                    link(v.tensor_scalar(qsc[:, a, w, :], qsc[:, a, w, :], col(IQ + a), None, ALU.mult))
                    link(v.tensor_tensor(tab[:, a, :, :], tab[:, a, :, :],
                                         qsc[:, a, w, :].unsqueeze(1).to_broadcast([P, TT, HD]), ALU.mult))
            dve.wait_ge(s["setup_a"], 1)
            v.tensor_scalar(aneg[:, :, :], aneg[:, :, :], -1.0, None, ALU.mult).then_inc(s["setup_v"], 1)
            for f in range(8):
                dve.wait_ge(s["setup_t"], f + 1)
                if f < 4:
                    dst = w1t[:, f // 2, (f % 2) * 512:(f % 2) * 512 + 512]
                    v.tensor_copy(dst, psh[f][:, 0:512]).then_inc(s["setup_tev"], 1)
                else:
                    g = f - 4
                    v.tensor_copy(w2t[:, 2 * g:2 * g + 2, :],
                                  psh[f][:, 0:512].rearrange("p (a n) -> p a n", a=2)).then_inc(s["setup_tev"], 1)

            need_max = dve.value_load(big_logits[0:1, 0:1])

            def guard(b):
                n = HEADS * TT
                for j in range(n):
                    h, tt = j // TT, j % TT
                    dve.wait_ge(s["guard_s"], b * n + j + 1)
                    v.reduce_max(rowmax[:, tt * HEADS + h:tt * HEADS + h + 1], ps[:, j % 4, :], AX.X).then_inc(s["guard_m"], 1)
                dve.wait_ge(s["guard_m"], (b + 1) * n)
                v.tensor_scalar(qka[:, 0, :, SHIFT], rowmax[:, :], -1.0, None, ALU.mult).then_inc(s["guard_h"], 1)
                dve.wait_ge(s["guard_h"], b + 1)
                v.scalar_tensor_tensor(qka[:, 0, :, SHIFT + 1], rowmax[:, :], -1.0, qka[:, 0, :, SHIFT],
                                       ALU.mult, ALU.subtract).then_inc(s["guard_w"], 1)
                for j in range(4):
                    dve.wait_ge(s["guard_t"], b * 4 + j + 1)
                    v.tensor_copy(*qk_evac(j)).then_inc(s["guard_c"], 1)

            def layernorm(kind, b, src):
                i = ln_before(kind, b)
                for tt in range(TT):
                    ins = v.bn_stats(bnst[:, tt, :], src[:, tt, :])
                ins.then_inc(s["stats"], 1)
                dve.wait_ge(s["stats"], i + 1)
                stand_alone(dve)
                for tt in range(TT):
                    ins = v.bn_aggr(mv[:, tt, :], bnst[:, tt, :])
                ins.then_inc(s["mv"], 1)
                dve.wait_ge(s["rstd"], i + 1)
                for tt in range(TT):
                    ins = v.tensor_scalar(xn[:, tt, :], src[:, tt, :], mv[:, tt, 0:1], rstd[:, tt:tt + 1],
                                          ALU.subtract, ALU.mult)
                ins.then_inc(s["xn"], 1)
                dve.wait_ge(s["hi"], i + 1)
                v.tensor_tensor(xt_lo[:, :, :], ps[:, 6:8, :], xt_hi[:, :, :], ALU.subtract).then_inc(s["lo"], 1)

            def ffn(kind, b, src, dst):
                g = ffn_before(kind, b)
                for f in range(FC):
                    dve.wait_ge(s["hhi"], g * FC + f + 1)
                    v.tensor_tensor(h_lo[:, f, :], hid[:, f % 4, :], h_hi[:, f, :], ALU.subtract).then_inc(s["hlo"], 1)
                dve.wait_ge(s["down"], g + 1)
                dve.wait_ge(s["biased"], bias_before(kind, b) + 1)
                for tt in range(TT):
                    v.scalar_tensor_tensor(dst[:, tt, :], ps[:, 4 + tt, 0:DIM], col(INV_S), src[:, tt, :],
                                           ALU.mult, ALU.add).then_inc(s["fout"], 1)

            def scan_step(m, n):
                dve.wait_ge(s["decay"], m * NS + n + 1)
                dve.wait_ge(s["dbu"], m * NS + n + 1)
                flat = hst[:, n % HSLOTS, :, :].rearrange("p d t -> p (d t)")
                v.tensor_tensor_scan(flat, decay[:, n % 2, :, :].rearrange("p d t -> p (d t)"), flat, 0.0,
                                     ALU.mult, ALU.add).then_inc(s["scan"], 1)

            def acc_step(m, n):
                for tt in range(TT):
                    dve.wait_ge(s["htp"], (m * NS + n) * TT + tt + 1)
                    src = ps[:, 4 + tt % 2, :]
                    if n == 0:
                        ins = v.tensor_scalar(acc[:, tt, :], src, ctok[:, tt, n:n + 1], None, ALU.mult)
                    else:
                        ins = v.scalar_tensor_tensor(acc[:, tt, :], src, ctok[:, tt, n:n + 1], acc[:, tt, :],
                                                     ALU.mult, ALU.add)
                    ins.then_inc(s["accd"], 1)

            def group_out(b, g):
                dve.wait_ge(s["pv"], b * PVS + 2 * g + 2)
                if g >= 1:
                    dve.wait_ge(s["otp"], b * NG + g)
                v.tensor_copy(ot, ps[:, 6, :]).then_inc(s["oev"], 1)

            def group_norm(b, g):
                dve.wait_ge(s["otp"], b * NG + g + 1)
                o4 = ps[:, 7, :].rearrange("p (t j r) -> p t j r", t=TT, j=GROUP)
                v.reciprocal(rden[:, :, :], o4[:, :, :, HD]).then_inc(s["rden"], 1)
                dve.wait_ge(s["rden"], b * NG + g + 1)
                v.tensor_tensor(on[:, :, g * GROUP * HD:(g + 1) * GROUP * HD].rearrange("p t (j d) -> p t j d", j=GROUP),
                                o4[:, :, :, 0:HD], rden[:, :, :].unsqueeze(3).to_broadcast([P, TT, GROUP, HD]),
                                ALU.mult).then_inc(s["on"], 1)

            def body(b, has_a, has_m):
                m = b - 1
                if has_a:
                    dve.wait_ge(s["ld_x"], 16 * (b + 1))
                    layernorm("attn", b, xa)
                    for tt in range(TT):
                        dve.wait_ge(s["qkv"], b * TT + tt // 2 * 2 + 2)
                        bank, o = 4 + tt // 2, (tt % 2) * DIM
                        v.tensor_scalar(vaug[:, tt, :, 0:HD], ps[:, bank, o:o + DIM].rearrange("p (h d) -> p h d", d=HD),
                                        col(A_QKV), None, ALU.mult).then_inc(s["vev"], 1)
                    dve.wait_ge(s["msq_sq"], (b + 1) * TT)
                    v.tensor_reduce(msq[:, :], sq.rearrange("p (a d) -> p a d", d=HD), AX.X, ALU.add).then_inc(s["msq_red"], 1)
                    dve.wait_ge(s["qn"], b + 1)
                    v.tensor_tensor(heads_view(sq), heads_view(qn), ropec[:, :, :, :].rearrange("p a b d -> p (a b) d").unsqueeze(2)
                                    .to_broadcast([P, 2 * TT, HEADS, HD]), ALU.mult).then_inc(s["ropea"], 1)
                    dve.wait_ge(s["rot_s"], 2 * (b + 1))
                    dve.wait_ge(s["ropea"], b + 1)
                    v.tensor_tensor(rot, sq, rot, ALU.add).then_inc(s["roped"], 1)
                    dve.wait_ge(s["roped"], b + 1)
                    v.memset(qka[:, 0, :, SHIFT:ROWS], 0.0)
                    v.memset(qka[:, 1, :, SHIFT:ROWS], 1.0)
                    dve.wait_ge(s["qhi"], 4 * (b + 1))
                    for a in range(2):
                        o = (1 + a) * HD
                        src = rot[:, a * TT * DIM:(a + 1) * TT * DIM].rearrange("p (h d) -> p h d", d=HD)
                        v.tensor_tensor(qka[:, a, :, o:o + HD], src, qka[:, a, :, 0:HD], ALU.subtract).then_inc(s["qlo"], 1)
                    for j in range(1, 8, 2):
                        dve.wait_ge(s["qktp"], b * 8 + j + 1)
                        v.tensor_copy(*qk_evac(j)).then_inc(s["qktv"], 1)
                    with dve.If(need_max == 1):
                        guard(b)
                    with dve.Else():
                        dve.sem_inc(s["waited"], 1)
                for n in range(NS + 1):
                    if has_m:
                        if n < NS:
                            scan_step(m, n)
                        if n >= 1:
                            acc_step(m, n - 1)
                    if has_a and n > GROUP and n % GROUP == 1:
                        group_norm(b, n // GROUP - 1)
                    if has_a and n >= GROUP and n % GROUP == 0:
                        group_out(b, n // GROUP - 1)
                if has_a:
                    group_norm(b, NG - 1)
                if has_m:
                    for d in range(DT):
                        dve.wait_ge(s["ytp"], m * DT + d + 1)
                        v.scalar_tensor_tensor(ybuf[:, d, :], u[:, d, :], dskip[:, d:d + 1], ps[:, d, :],
                                               ALU.mult, ALU.add).then_inc(s["yskip"], 1)
                        dve.wait_ge(s["yskip"], m * DT + d + 1)
                        v.tensor_tensor(ybuf[:, d, :], ybuf[:, d, :], sres[:, d, :], ALU.mult).then_inc(s["y"], 1)
                    dve.wait_ge(s["biased"], b * 4 - 1)
                    for tt in range(TT):
                        dve.wait_ge(s["wo"], m * TT + tt // 2 * 2 + 2)
                        ins = v.tensor_tensor(xb[:, tt, :], ps[:, 4 + tt // 2, (tt % 2) * DIM:(tt % 2 + 1) * DIM],
                                              xb[:, tt, :], ALU.add)
                        ins.then_inc(s["woev"], 1)
                    dve.wait_ge(s["woev"], b * TT)
                    layernorm("ffn2", b, xb)
                    dve.wait_ge(s["store"], 16 * b)
                    ffn("ffn2", b, xb, yo)
                if has_a:
                    dve.wait_ge(s["biased"], bias_before("attn", b) + 1)
                    for tt in range(TT):
                        dve.wait_ge(s["proj"], b * TT + tt // 2 * 2 + 2)
                        v.tensor_tensor(xa[:, tt, :], ps[:, 2 + tt // 2, (tt % 2) * DIM:(tt % 2 + 1) * DIM],
                                        xa[:, tt, :], ALU.add).then_inc(s["pjev"], 1)
                    dve.wait_ge(s["pjev"], (b + 1) * TT)
                    layernorm("ffn1", b, xa)
                    ffn("ffn1", b, xa, xb)
                    dve.wait_ge(s["fout"], (ffn_before("ffn1", b) + 1) * TT)
                    layernorm("scan", b, xb)
                    v.memset(xpad[:, :, 0:1], 0.0)
                    v.memset(xpad[:, :, 1 + SEQ:SEQ + CONV - 1], 0.0)
                    for d in range(DT):
                        dve.wait_ge(s["xin"], b * DT + d + 1)
                        pad = xpad[:, d % 2, :]
                        v.tensor_scalar(pad[:, 1:1 + SEQ], ps[:, X_BANK[d], :], col(A_IN), None, ALU.mult).then_inc(s["xpad"], 1)
                        dve.wait_ge(s["xpad"], b * DT + d + 1)
                        cv = hst[:, 0, d, :]
                        nstep = CONV - 1
                        v.tensor_scalar(cv, pad[:, 0:SEQ], kconv[:, d, 0:1], None, ALU.mult).then_inc(s["conv1"], 1)
                        for j in range(1, CONV):
                            dve.wait_ge(s["conv1"], (b * DT + d) * nstep + j)
                            ins = v.scalar_tensor_tensor(cv, pad[:, j:j + SEQ], kconv[:, d, j:j + 1], cv, ALU.mult, ALU.add)
                            ins.then_inc(s["conv1"] if j < nstep else s["conv"], 1)
                        dve.wait_ge(s["dtp"], b * DT + d + 1)
                        v.tensor_scalar(hst[:, 1, d, :], ps[:, DT_BANK[d], :], bdt[:, d:d + 1], 30.0, ALU.add, ALU.min).then_inc(s["zc"], 1)
                    for d in range(DT):
                        dve.wait_ge(s["lz"], b * DT + d + 1)
                        v.scalar_tensor_tensor(delta[:, d, :], ps[:, DT_BANK[d], :], bdt[:, d:d + 1], hst[:, 1, d, :],
                                               ALU.add, ALU.max).then_inc(s["delta"], 1)
                    dve.wait_ge(s["ctp"], b + 1)
                    v.tensor_copy(ctok[:, :, :], ps[:, 5, :].rearrange("p (t r) -> p t r", t=TT)[:, :, RANK + NS:XD]).then_inc(s["cev"], 1)

            iterations(dve, body)

        @block.tensor
        def _(pe):
            mm, tp = nc.tensor.matmul, nc.tensor.transpose
            pe.wait_ge(s["setup_p"], 7)
            pe.wait_ge(s["setup_v"], 1)
            tp(ps[0:8, 0, 0:P], sc[:, 0:8], identf[:, :]).then_inc(s["setup_r"], 1)
            pe.wait_ge(s["setup_v"], 2)
            mm(ps[:, 1, 0:16], ones8[:, :], reddiag[:, :], start=True, stop=True).then_inc(s["setup_r"], 1)
            pe.wait_ge(s["setup_v"], 3)
            for f in range(4):
                c, base = f // 2, (f % 2) * 4
                for i in range(4):
                    ins = tp(psh[f][:, i * P:(i + 1) * P], tern1[:, base + i, c * P:(c + 1) * P], identh[:, :])
                ins.then_inc(s["setup_t"], 1)
            for g in range(4):
                for i in range(4):
                    ins = tp(psh[4 + g][:, i * P:(i + 1) * P],
                             tern2[:, i % 2, (2 * g + i // 2) * P:(2 * g + i // 2 + 1) * P], identh[:, :])
                ins.then_inc(s["setup_t"], 1)
            pe.wait_ge(s["setup_tev"], 8)

            need_max = pe.value_load(big_logits[0:1, 0:1])

            def q_or_k_transposes(j):
                bank = QK_BANK[j]
                for e in range(2):
                    hp = (j % 4) * 2 + e
                    for tt in range(TT):
                        o = e * SEQ + tt * P
                        src = qka[:, j // 4, tt * HEADS + 2 * hp:tt * HEADS + 2 * hp + 2, :].rearrange("p h r -> p (h r)")
                        ins = tp(psh[bank][:, o:o + P], src, identh[:, :])
                return ins

            def guard(b):
                n = HEADS * TT
                for j in range(n):
                    h, tt = j // TT, j % TT
                    r, hp = (h % 2) * ROWS, h // 2
                    if j >= 4:
                        pe.wait_ge(s["guard_m"], b * n + j - 3)
                    mm(ps[:, j % 4, :], qt[r:r + ROWS, hp, tt * P:(tt + 1) * P], kt[r:r + ROWS, hp, :],
                       start=True, stop=True).then_inc(s["guard_s"], 1)
                pe.wait_ge(s["guard_w"], b + 1)
                for j in range(4):
                    q_or_k_transposes(j).then_inc(s["guard_t"], 1)
                pe.wait_ge(s["guard_c"], 4 * (b + 1))

            def layernorm(kind, b):
                i = ln_before(kind, b)
                pe.wait_ge(s["xn"], i + 1)
                for c in range(KC):
                    for tt in range(TT):
                        ins = tp(ps[:, 6 + c, tt * P:(tt + 1) * P], xn[:, tt, c * P:(c + 1) * P], identf[:, :])
                ins.then_inc(s["xt"], 1)
                pe.wait_ge(s["lo"], i + 1)

            def ffn(kind, b):
                g = ffn_before(kind, b)

                def up(f):
                    if f >= 4:
                        pe.wait_ge(s["hid"], g * FC + f - 3)
                    for c in range(KC):
                        for part in (xt_hi, xt_lo):
                            ins = mm(ps[:, f % 4, :], w1t[:, c, f * P:(f + 1) * P], part[:, c, :],
                                     start=(c == 0 and part is xt_hi), stop=(c == KC - 1 and part is xt_lo))
                    ins.then_inc(s["up"], 1)

                def down(f):
                    pe.wait_ge(s["hlo"], g * FC + f + 1)
                    for tt in range(TT):
                        for part in (h_hi, h_lo):
                            ins = mm(ps[:, 4 + tt, 0:DIM], part[:, f, tt * P:(tt + 1) * P], w2t[:, f, :],
                                     start=(f == 0 and part is h_hi), stop=(f == FC - 1 and part is h_lo))
                    return ins

                for f in range(FC + 2):
                    if f < FC:
                        up(f)
                    if f >= 2:
                        ins = down(f - 2)
                ins.then_inc(s["down"], 1)

            def split_mm(dst, w_hi, w_lo, w_is_lhs, xs, ws):
                n = 0
                for c in range(KC):
                    for xp, wp in ((xt_hi, w_hi), (xt_hi, w_lo), (xt_lo, w_hi)):
                        xo, wo_ = xp[(slice(None), c) + xs], wp[(slice(None), c) + ws]
                        a, bb = (wo_, xo) if w_is_lhs else (xo, wo_)
                        ins = mm(dst, a, bb, start=(n == 0), stop=(n == 3 * KC - 1))
                        n += 1
                return ins

            def body(b, has_a, has_m):
                m = b - 1
                if has_a:
                    if has_m:
                        pe.wait_ge(s["delta"], b * DT)
                        pe.wait_ge(s["sres_"], b * DT)
                        pe.wait_ge(s["cev"], b)
                    layernorm("attn", b)
                    for tt in range(TT):
                        xs = (slice(tt * P, (tt + 1) * P),)
                        split_mm(ps[:, tt, :], wqkv_hi, wqkv_lo, False, xs, (slice(0, 2 * DIM),))
                        ins = split_mm(ps[:, 4 + tt // 2, (tt % 2) * DIM:(tt % 2 + 1) * DIM], wqkv_hi, wqkv_lo, False, xs,
                                       (slice(2 * DIM, 3 * DIM),))
                        ins.then_inc(s["qkv"], 1)
                    pe.wait_ge(s["qlo"], 2 * (b + 1))
                    pe.wait_ge(s["msq_sq"], (b + 1) * TT)
                    for j in range(8):
                        if j >= 6:
                            pe.wait_ge(s["qkta"] if j % 2 == 0 else s["qktv"], b * 4 + 1)
                        q_or_k_transposes(j).then_inc(s["qktp"], 1)
                    pe.wait_ge(s["qkta"], 4 * (b + 1))
                    pe.wait_ge(s["qktv"], 4 * (b + 1))
                    pe.wait_ge(s["vev"], TT * (b + 1))
                    with pe.If(need_max == 1):
                        guard(b)
                    with pe.Else():
                        pe.sem_inc(s["waited"], 1)
                elif has_m:
                    pe.wait_ge(s["delta"], b * DT)
                    pe.wait_ge(s["sres_"], b * DT)
                    pe.wait_ge(s["cev"], b)
                def scores(i):
                    h, k0 = unit(i)
                    r, hp = (h % 2) * ROWS, h // 2
                    if i >= 2:
                        pe.wait_ge(s["prob"], b * UNITS + i - 1)
                    for kk in range(2):
                        ins = mm(ps[:, 2 * (i % 2) + kk, :], kt[r:r + ROWS, hp, (k0 + kk) * P:(k0 + kk + 1) * P],
                                 qt[r:r + ROWS, hp, :], start=True, stop=True)
                    ins.then_inc(s["score"], 1)

                def values(k):
                    g, pair = k // 2, k % 2
                    pe.wait_ge(s["prob"], b * UNITS + GROUP * (k + 1))
                    if pair == 0 and g >= 1:
                        pe.wait_ge(s["oev"], b * NG + g)
                    for kk in range(2):
                        for j in range(GROUP):
                            kc = 2 * pair + kk
                            ins = mm(ps[32 * j:32 * j + 32, 6, :], vaug[:, kc, g * GROUP + j, :],
                                     prob[:, (k * GROUP + j) % PSLOTS, kk, :], start=(kc == 0), stop=(kc == TT - 1))
                    ins.then_inc(s["pv"], 1)

                def out_rows(g):
                    pe.wait_ge(s["oev"], b * NG + g + 1)
                    if g >= 1:
                        pe.wait_ge(s["on"], b * NG + g)
                    for tt in range(TT):
                        ins = tp(ps[:, 7, tt * P:(tt + 1) * P], ot[:, tt * P:(tt + 1) * P], identf[:, :])
                    ins.then_inc(s["otp"], 1)

                def states(n, tiles):
                    pe.wait_ge(s["scan"], m * NS + n + 1)
                    for tt in tiles:
                        if n * TT + tt >= 2:
                            pe.wait_ge(s["accd"], (m * NS + n) * TT + tt - 1)
                        for d in range(DT):
                            ins = tp(ps[:, 4 + tt % 2, d * P:(d + 1) * P], hst[:, n % HSLOTS, d, tt * P:(tt + 1) * P], identf[:, :])
                        ins.then_inc(s["htp"], 1)

                for n in range(NS + 1):
                    if has_a and n < NS:
                        scores(2 * n)
                    if has_m and n < NS:
                        states(n, (0, 1))
                    if has_a and n < NS:
                        scores(2 * n + 1)
                    if has_a and n >= 2 and n % 2 == 0:
                        values(n // 2 - 1)
                    if has_m and n < NS:
                        states(n, (2, 3))
                    if has_a and n >= GROUP and n % GROUP == 0:
                        out_rows(n // GROUP - 1)
                if has_m:
                    pe.wait_ge(s["accd"], b * NS * TT)
                    for d in range(DT):
                        for tt in range(TT):
                            ins = tp(ps[:, d, tt * P:(tt + 1) * P], acc[:, tt, d * P:(d + 1) * P], identf[:, :])
                        ins.then_inc(s["ytp"], 1)
                    pe.wait_ge(s["y"], b * DT)
                    for tt in range(TT):
                        for d in range(DT):
                            ins = mm(ps[:, 4 + tt // 2, (tt % 2) * DIM:(tt % 2 + 1) * DIM],
                                     ybuf[:, d, tt * P:(tt + 1) * P], wout[:, d, :], start=(d == 0), stop=(d == DT - 1))
                        ins.then_inc(s["wo"], 1)
                    if has_a:
                        pe.wait_ge(s["on"], (b + 1) * NG)
                    layernorm("ffn2", b)
                    ffn("ffn2", b)
                if has_a:
                    pe.wait_ge(s["on"], (b + 1) * NG)
                    for c in range(KC):
                        for tt in range(TT):
                            ins = tp(ps[:, c, tt * P:(tt + 1) * P], on[:, tt, c * P:(c + 1) * P], identf[:, :])
                    ins.then_inc(s["ontp"], 1)
                    pe.wait_ge(s["ocev"], b + 1)
                    for tt in range(TT):
                        for c in range(KC):
                            ins = mm(ps[:, 2 + tt // 2, (tt % 2) * DIM:(tt % 2 + 1) * DIM],
                                     oc[:, c, tt * P:(tt + 1) * P], wproj[:, c, :], start=(c == 0), stop=(c == KC - 1))
                        ins.then_inc(s["proj"], 1)
                    if has_m:
                        pe.wait_ge(s["fout"], 2 * b * TT)
                    layernorm("ffn1", b)
                    ffn("ffn1", b)
                    layernorm("scan", b)
                    split_mm(ps[0:XD, 0, :], wx_hi, wx_lo, True, (slice(None),), (slice(0, XD),)).then_inc(s["xdp"], 1)
                    for d in range(DT):
                        split_mm(ps[:, X_BANK[d], :], win_hi, win_lo, True, (slice(None),),
                                 (slice(d * P, (d + 1) * P),)).then_inc(s["xin"], 1)
                    pe.wait_ge(s["xdev"], b + 1)
                    for d in range(DT):
                        ins = split_mm(ps[:, RES_BANK[d], :], win_hi, win_lo, True, (slice(None),),
                                       (slice(D_INNER + d * P, D_INNER + (d + 1) * P),))
                        ins.then_inc(s["res"], 1)
                    for d in range(DT):
                        pe.wait_ge(s["xpad"], b * DT + d + 1)
                        mm(ps[:, DT_BANK[d], :], wdt[:, d * P:(d + 1) * P], xdbl[0:RANK, :], start=True,
                           stop=True).then_inc(s["dtp"], 1)
                    pe.wait_ge(s["sres_"], b * DT + 1)
                    for tt in range(TT):
                        ins = tp(ps[:, 5, tt * P:tt * P + XD], xdbl[:, tt * P:(tt + 1) * P], identf[0:XD, 0:XD])
                    ins.then_inc(s["ctp"], 1)

            iterations(pe, body)


_INS = ['L0_attn_a_x', 'L0_attn_a_w_qkv', 'L0_attn_a_q_scale', 'L0_attn_a_k_scale', 'L0_attn_a_w_proj',
        'L0_attn_a_b_proj', 'L0_attn_b_W_in', 'L0_attn_b_K_conv', 'L0_attn_b_b_conv', 'L0_attn_b_W_x',
        'L0_attn_b_W_dt', 'L0_attn_b_b_dt', 'L0_attn_b_A_log', 'L0_attn_b_D', 'L0_attn_b_W_out',
        'L0_attn_b_b_out', 'L0_ffn_W1', 'L0_ffn_b1', 'L0_ffn_W2', 'L0_ffn_b2']


def rope_tables():
    import numpy as _np
    freqs = (1.0 / _np.float32(2500) ** (_np.arange(HALF, dtype=_np.float32) / HALF)).astype(_np.float32)
    angle = _np.outer(_np.arange(SEQ, dtype=_np.float32), freqs).astype(_np.float32).astype(_np.float64)
    cos, sin = _np.cos(angle), _np.sin(angle)
    return (_np.concatenate([cos, cos], 1).astype(_np.float32), _np.concatenate([-sin, sin], 1).astype(_np.float32))


def kernel(**inputs):
    import numpy as _np
    import concourse.bacc as _bacc
    from concourse.bass_utils import run_bass_kernel_spmd as _run

    nc = _bacc.Bacc("TRN2", target_bir_lowering=False, num_devices=1)
    arrays, aps = {}, {}
    for name in _INS:
        a = _np.ascontiguousarray(inputs[name])
        arrays["in_" + name] = a
        aps[name] = nc.dram_tensor("in_" + name, a.shape, mybir.dt.from_np(a.dtype), kind="ExternalInput").ap()
    tables = []
    for name, a in zip(("rope_cos", "rope_sin"), rope_tables()):
        arrays[name] = a
        tables.append(nc.dram_tensor(name, a.shape, mybir.dt.from_np(a.dtype), kind="ExternalInput").ap())
    bt = nc.dram_tensor("b_rows", (NS, SEQ), FP32, kind="Internal").ap()
    out = nc.dram_tensor("out_0", (BATCH, SEQ, DIM), FP32, kind="ExternalOutput").ap()
    hybrid_block(nc, aps, out, tables[0], tables[1], bt)
    r = _run(nc, [arrays], core_ids=[0])
    return r.results[0]["out_0"]
```

```python
import numpy as np
import concourse.bass as bass
from concourse import mybir
from contextlib import ExitStack

FP32 = mybir.dt.float32
FP16 = mybir.dt.float16
ALU = mybir.AluOpType
ACT = mybir.ActivationFunctionType
AX = mybir.AxisListType

BATCH, SEQ, DIM = 8, 512, 256
P = 128
TT = SEQ // P
KC = DIM // P
HEADS = 16
HD = DIM // HEADS
HALF = HD // 2
ROWS = 64
D_INNER = 512
DT = D_INNER // P
NS = 16
RANK = 64
XD = RANK + 2 * NS
FF = 1024
FC = FF // P
CONV = 4
LN_EPS = 1e-5
RMS_EPS = 1e-6
EXP_LN = "natural_log_exp_and_others"
Q_EPS = 1e-5
SHIFT = 3 * HD
GROUP = 4
PSLOTS = 8
HSLOTS = 3
LN_BOUND = 256.0
MAX_LOGIT_UNSHIFTED = 60.0


def hybrid_block(nc, t, out, cos_t, sin_t, bt_scratch):
    x_d, y_d = t["L0_attn_a_x"], out

    with ExitStack() as ctx:
        def sb(name, shape, dt=FP32):
            return ctx.enter_context(nc.sbuf_tensor(name, shape, dt))

        def sem(name):
            return ctx.enter_context(nc.semaphore(name))

        wqkv_hi = sb("wqkv_hi", [P, KC, 3 * DIM], FP16)
        wqkv_lo = sb("wqkv_lo", [P, KC, 3 * DIM], FP16)
        win_hi = sb("win_hi", [P, KC, 2 * D_INNER], FP16)
        win_lo = sb("win_lo", [P, KC, 2 * D_INNER], FP16)
        wx_hi = sb("wx_hi", [P, KC, XD], FP16)
        wx_lo = sb("wx_lo", [P, KC, XD], FP16)
        wdt = sb("wdt", [RANK, D_INNER])
        wproj = sb("wproj", [P, KC, DIM])
        wout = sb("wout", [P, DT, DIM])
        w1t = sb("w1t", [P, KC, FF], FP16)
        w2t = sb("w2t", [P, FC, DIM], FP16)
        bproj = sb("bproj", [P, DIM])
        bout = sb("bout", [P, DIM])
        b2 = sb("b2", [P, DIM])
        b1 = sb("b1", [P, FC])
        bdt = sb("bdt", [P, DT])
        bconv = sb("bconv", [P, DT])
        dskip = sb("dskip", [P, DT])
        kconv = sb("kconv", [P, DT, CONV])
        aneg = sb("aneg", [P, DT, NS])
        ropec = sb("ropec", [P, 2, TT, HD])
        ropes = sb("ropes", [P, 2, TT, HD])
        identf = sb("identf", [P, P])
        identh = sb("identh", [P, P], FP16)
        sc = sb("sc", [P, 32])
        big_logits = sb("big_logits", [P, 1], mybir.dt.uint32)
        rowmax = sb("rowmax", [P, TT * HEADS])
        ones8 = sb("ones8", [8, P])
        red = sb("red", [8, 2])
        reddiag = sb("reddiag", [8, 16])
        xa = sb("xa", [P, TT, DIM])
        xb = sb("xb", [P, TT, DIM])
        yo = sb("yo", [P, TT, DIM])
        xn = sb("xn", [P, TT, DIM])
        bnst = sb("bnst", [P, 2, TT, 6])
        mv = sb("mv", [P, 2, TT, 2])
        lnv = sb("lnv", [P, 2, TT])
        rstd = sb("rstd", [P, 2, TT])
        xt_a = sb("xt_a", [P, 2, KC, SEQ], FP16)
        qt = sb("qt", [P, HEADS // 2, SEQ], FP16)
        kt = sb("kt", [P, HEADS // 2, SEQ], FP16)
        vaug = sb("vaug", [P, TT, HEADS, 2 * HD])
        ot = xn[:, 0:2, :].rearrange("p a n -> p (a n)")
        rden = sb("rden", [P, TT, GROUP])
        on = sb("on", [P, TT, DIM])
        msq = sb("msq", [P, 2 * TT * HEADS])
        rms = sb("rms", [P, 2 * TT * HEADS])
        delta = sb("delta", [P, DT, SEQ])
        u = sb("u", [P, DT, SEQ])
        du = sb("du", [P, DT, SEQ])
        sres = sb("sres", [P, DT, SEQ])
        xdbl = sb("xdbl", [XD, SEQ])
        ctok = sb("ctok", [P, TT, NS])
        acc = sb("acc", [P, TT, D_INNER])
        decay = sb("decay", [P, 2, DT, SEQ])
        hst = sb("hst", [P, HSLOTS, DT, SEQ])
        bbc = sb("bbc", [P, 2, SEQ])
        ybuf = delta
        convtmp = hst[:, 1, :, :]
        xpad = acc[:, :, :].rearrange("p (i a) n -> p i (a n)", i=2)[:, :, 0:SEQ + CONV - 1]
        arena = sb("arena", [P, PSLOTS * 2 * SEQ])
        prob = arena[:, :].rearrange("p (s k q) -> p s k q", s=PSLOTS, k=2)
        W = TT * SEQ
        qk = arena[:, 0:W].rearrange("p (a n) -> p a n", a=2 * TT)
        sq = arena[:, W:2 * W]
        qn = arena[:, 2 * W:3 * W]
        rot = arena[:, 3 * W:4 * W]
        qka = arena[:, 0:2 * W].bitcast(FP16).rearrange("p (a h r) -> p a h r", h=TT * HEADS, r=ROWS)
        def hidden(space):
            return (space[:, 0:W].rearrange("p (s n) -> p s n", s=4),
                    space[:, W:2 * W].bitcast(FP16).rearrange("p (f n) -> p f n", f=FC),
                    space[:, 2 * W:3 * W].bitcast(FP16).rearrange("p (f n) -> p f n", f=FC))

        hstf = hst[:, :, :, :].rearrange("p s d t -> p (s d t)")
        HIDDEN = {1: hidden(hstf), 2: hidden(arena)}
        oc = hstf[:, 2 * W:2 * W + KC * SEQ].rearrange("p (c n) -> p c n", c=KC)
        xt_b = qt[:, 0:4, :].rearrange("p (h c) n -> p h c n", h=2)
        LN = {"a": (0, xn, xt_a, (0, 1)), "b": (1, on, xt_b, (4, 5))}
        ldq = arena[:, 0:KC * 3 * DIM].rearrange("p (c n) -> p c n", c=KC)
        ldi = arena[:, 1536:1536 + KC * 2 * D_INNER].rearrange("p (c n) -> p c n", c=KC)
        ldx = arena[:, 3584:3584 + KC * XD].rearrange("p (c n) -> p c n", c=KC)
        ldw1 = sres[:, :, :].rearrange("p a n -> p (a n)").rearrange("p (f n) -> p f n", f=FC)
        ldw2 = u[:, :, :].rearrange("p a n -> p (a n)").rearrange("p (c n) -> p c n", c=KC)
        accf = acc[:, :, :].rearrange("p a n -> p (a n)")
        tern1 = accf[:, 0:1024].bitcast(FP16).rearrange("p (f n) -> p f n", f=FC)
        tern2 = accf[:, 1024:2048].bitcast(FP16).rearrange("p (c n) -> p c n", c=KC)
        stmp = du[:, :, :].rearrange("p a n -> p (a n)")
        qsc = sb("qsc", [P, 2, 2, HD])

        ps = ctx.enter_context(nc.psum_tensor("ps", [P, 8, SEQ], FP32))
        psh = [ps[:, i, :].bitcast(FP16) for i in range(8)]

        (A_QKV, A_IN, A_X, G1, G2, MQ, MK, MB, I_QKV, I_IN, I_X, TH1, TH2, NTH1, NTH2, LOGIT, S_H,
         INV_S, EPS_LN, EPS_RMS, IQ, IK, TMP, R0, R1) = range(25)

        def col(i, n=1):
            return sc[:, i:i + n]

        UNITS = 2 * HEADS
        NG = HEADS // GROUP
        PVS = UNITS // GROUP

        def unit(i):
            g, pair, j = i // (2 * GROUP), i // GROUP % 2, i % GROUP
            return g * GROUP + j, 2 * pair

        QK_BANK = [0, 1, 2, 3, 0, 1, 2, 3]
        V_BANK, QKV_BANK = [2, 2, 3, 3], [0, 1, 2, 3]
        WX_BANK, X_BANK, RES_BANK, C_BANK, DT_BANK = 4, [5, 6, 7, 4], [5, 6, 7, 4], 5, [6, 7, 4, 5]
        n_loads = [0]

        def stand_alone(eng):
            eng.sem_inc(s["waited"], 1)

        def qk_evac(j):
            dst = (qt, kt)[j // 4]
            return dst[:, (j % 4) * 2:(j % 4) * 2 + 2, :], psh[QK_BANK[j]].rearrange("p (a n) -> p a n", a=2)

        def tile_bank(bank, tt):
            return ps[:, bank + tt // 2, (tt % 2) * DIM:(tt % 2 + 1) * DIM]

        def heads_view(flat):
            return flat.rearrange("p (a h d) -> p a h d", a=2 * TT, d=HD)

        names = """ld_w ld_x setup_v setup_p setup_a setup_r setup_t setup_tev setup_ev
                   stats_a mv_a lnv_a rstd_a xn_a xt_a hi_a lo_a stats_b mv_b lnv_b rstd_b xn_b xt_b hi_b lo_b
                   bias_proj bias_f1 bias_f2 bias_out
                   qkv qkv_v qkev vev msq_sq msq_red msq_ln msq_rs qn rot_s ropea roped qhi qlo qktp qkta qktv
                   guard_s guard_m guard_h guard_w guard_t guard_c
                   score prob pv oev otp rden on
                   decay dbu scan htp accd bload0 bload1 bstore
                   ytp yskip y wo woev ontp ocev proj pjev
                   up1 hid1 hhi1 hlo1 down1 fout1 up2 hid2 hhi2 hlo2 down2 fout2
                   xdp xdev ctp cev dtp zc ez lz delta xin xpad conv1 conv uu res rescp sres_ du store waited
                   """.split()
        s = {n: sem("s_" + n) for n in names}

        block = ctx.enter_context(nc.Block())

        def iterations(eng, pre, body):
            pre(0)
            body(0, True, False, True)
            with eng.Fori(1, BATCH - 1) as b:
                body(b, True, True, True)
            body(BATCH - 1, True, True, False)
            body(BATCH, False, True, False)

        def ln_set(kind, b):
            if kind == "attn":
                return "a", 0 if isinstance(b, int) and b == 0 else b * 2 - 1
            if kind == "ffn2":
                return "a", BATCH * 2 - 1 if isinstance(b, int) and b == BATCH else b * 2
            return "b", b * 2 if kind == "ffn1" else b * 2 + 1

        @block.sync
        def _(sp):
            first = [
                (ldq, t["L0_attn_a_w_qkv"].rearrange("(c p) n -> p c n", p=P)),
                (ldi, t["L0_attn_b_W_in"].rearrange("(c p) n -> p c n", p=P)),
                (ldx, t["L0_attn_b_W_x"].rearrange("(c p) n -> p c n", p=P)),
                (ldw1, t["L0_ffn_W1"].rearrange("(f p) n -> p f n", p=P)),
                (ldw2, t["L0_ffn_W2"].rearrange("(c p) n -> p c n", p=P)),
                (wdt[:, :], t["L0_attn_b_W_dt"]),
                (wproj[:, :, :], t["L0_attn_a_w_proj"].rearrange("(c p) n -> p c n", p=P)),
                (wout[:, :, :], t["L0_attn_b_W_out"].rearrange("(c p) n -> p c n", p=P)),
                (bproj[:, :], t["L0_attn_a_b_proj"].partition_broadcast(P)),
                (bout[:, :], t["L0_attn_b_b_out"].partition_broadcast(P)),
                (b2[:, :], t["L0_ffn_b2"].partition_broadcast(P)),
                (qsc[:, 0, 0, :], t["L0_attn_a_q_scale"].partition_broadcast(P)),
                (qsc[:, 1, 0, :], t["L0_attn_a_k_scale"].partition_broadcast(P)),
                (ropec[:, 0, :, :], cos_t.rearrange("(a p) n -> p a n", p=P)),
                (ropec[:, 1, :, :], cos_t.rearrange("(a p) n -> p a n", p=P)),
                (ropes[:, 0, :, :], sin_t.rearrange("(a p) n -> p a n", p=P)),
                (ropes[:, 1, :, :], sin_t.rearrange("(a p) n -> p a n", p=P)),
                (aneg[:, :, :], t["L0_attn_b_A_log"].rearrange("(c p) n -> p c n", p=P)),
            ]
            for a in range(2):
                name = "L0_attn_a_q_scale" if a == 0 else "L0_attn_a_k_scale"
                for half in range(2):
                    first.append((qsc[:, a, 1, half * HALF:(half + 1) * HALF],
                                  t[name][(1 - half) * HALF:(2 - half) * HALF].partition_broadcast(P)))
            with nc.allow_non_contiguous_dma(reason="small vectors laid over partitions, once"):
                slow = [
                    (b1[:, :], t["L0_ffn_b1"].rearrange("(f p) -> p f", p=P)),
                    (bdt[:, :], t["L0_attn_b_b_dt"].rearrange("(f p) -> p f", p=P)),
                    (bconv[:, :], t["L0_attn_b_b_conv"].rearrange("(f p) -> p f", p=P)),
                    (dskip[:, :], t["L0_attn_b_D"].rearrange("(f p) -> p f", p=P)),
                ] + [(kconv[:, :, j], t["L0_attn_b_K_conv"][j, 0, :].rearrange("(f p) -> p f", p=P))
                     for j in range(CONV)]
                for dst, src in first + slow:
                    sp.dma_start(dst, src).then_inc(s["ld_w"], 16)
            n_loads[0] = len(first + slow)

            def load_b_row(m, n):
                if n >= 2:
                    sp.wait_ge(s["dbu"], m * NS + n - 1)
                    stand_alone(sp)
                sp.dma_start(bbc[:, n % 2, :], bt_scratch[n, :].partition_broadcast(P)).then_inc(s[("bload0", "bload1")[n % 2]], 16)

            def load_x(b):
                sp.dma_start(xa[:, :, :], x_d[b].rearrange("(a p) n -> p a n", p=P)).then_inc(s["ld_x"], 16)

            def body(b, has_a, has_m, has_next):
                if has_m:
                    sp.wait_ge(s["bstore"], b * 16)
                    stand_alone(sp)
                    for n in range(NS):
                        load_b_row(b - 1, n)
                if has_next:
                    sp.wait_ge(s["fout1"], (b + 1) * TT)
                    stand_alone(sp)
                    load_x(b + 1)
                if has_m:
                    sp.wait_ge(s["fout2"], b * TT)
                    stand_alone(sp)
                    sp.dma_start(y_d[b - 1].rearrange("(a p) n -> p a n", p=P), yo[:, :, :]).then_inc(s["store"], 16)
                if has_a:
                    sp.wait_ge(s["xdev"], b + 1)
                    stand_alone(sp)
                    if has_m:
                        sp.wait_ge(s["dbu"], b * NS)
                    sp.dma_start(bt_scratch[:, :], xdbl[RANK:RANK + NS, :]).then_inc(s["bstore"], 16)

            iterations(sp, load_x, body)
            sp.wait_ge(s["store"], 16 * (BATCH + 1))

        @block.gpsimd
        def _(pool):
            nc.gpsimd.memset(identf[:, :], 0.0).then_inc(s["setup_p"], 1)
            nc.gpsimd.memset(identh[:, :], 0.0).then_inc(s["setup_p"], 1)
            pool.wait_ge(s["setup_p"], 2)
            for m in (identf, identh):
                nc.gpsimd.affine_select(out=m[:, :], in_=m[:, :], compare_op=ALU.not_equal, fill=1.0,
                                        base=0, pattern=[[-1, P]], channel_multiplier=1).then_inc(s["setup_p"], 1)
            nc.gpsimd.memset(vaug[:, :, :, HD:2 * HD], 1.0).then_inc(s["setup_p"], 1)
            nc.gpsimd.memset(ones8[:, :], 1.0).then_inc(s["setup_p"], 1)
            nc.gpsimd.memset(decay[:, :, :, 0:1], 0.0).then_inc(s["setup_p"], 1)
            nc.gpsimd.memset(yo[:, 0, 0:1], 0.0).then_inc(s["store"], 16)

            def add_bias(dst, bias, kind, b, done):
                st, i = ln_set(kind, b)
                pool.wait_ge(s["xn_" + st], i + 1)
                nc.gpsimd.tensor_tensor(dst[:, :, :], dst[:, :, :],
                                        bias[:, :].unsqueeze(1).to_broadcast([P, TT, DIM]),
                                        ALU.add).then_inc(s[done], 1)

            def pre(b):
                add_bias(xa, bproj, "attn", b, "bias_proj")
                pool.wait_ge(s["msq_rs"], b + 1)
                nc.gpsimd.tensor_tensor(
                    qn.rearrange("p (a d) -> p a d", d=HD),
                    qk.rearrange("p a (h d) -> p (a h) d", d=HD),
                    rms[:, :].unsqueeze(2).to_broadcast([P, 2 * TT * HEADS, HD]), ALU.mult).then_inc(s["qn"], 1)
                pool.wait_ge(s["qn"], b + 1)
                s3 = ropes[:, :, :, :].rearrange("p a b d -> p (a b) d")
                for half in range(2):
                    to, frm = half * HALF, (1 - half) * HALF
                    nc.gpsimd.tensor_tensor(
                        heads_view(rot)[:, :, :, to:to + HALF], heads_view(qn)[:, :, :, frm:frm + HALF],
                        s3[:, :, to:to + HALF].unsqueeze(2).to_broadcast([P, 2 * TT, HEADS, HALF]),
                        ALU.mult).then_inc(s["rot_s"], 1)

            def body(b, has_a, has_m, has_next):
                if has_m:
                    pool.wait_ge(s["du"], b * DT)
                    for n in range(NS):
                        pool.wait_ge(s[("bload0", "bload1")[n % 2]], ((b - 1) * (NS // 2) + n // 2 + 1) * 16)
                        if n >= HSLOTS:
                            pool.wait_ge(s["htp"], ((b - 1) * NS + n - HSLOTS + 1) * TT)
                        nc.gpsimd.tensor_tensor(
                            hst[:, n % HSLOTS, :, :], du[:, :, :],
                            bbc[:, n % 2, :].unsqueeze(1).to_broadcast([P, DT, SEQ]), ALU.mult).then_inc(s["dbu"], 1)
                if has_a:
                    add_bias(xa, b2, "ffn1", b, "bias_f1")
                if has_m:
                    add_bias(yo, b2, "ffn2", b, "bias_f2")
                if has_a:
                    add_bias(xb, bout, "scan", b, "bias_out")
                if has_next:
                    pre(b + 1)
                if has_a:
                    for d in range(DT):
                        pool.wait_ge(s["delta"], b * DT + d + 1)
                        pool.wait_ge(s["uu"], b * DT + d + 1)
                        nc.gpsimd.tensor_tensor(du[:, d, :], delta[:, d, :], u[:, d, :], ALU.mult).then_inc(s["du"], 1)

            iterations(pool, pre, body)

        @block.scalar
        def _(act):
            nc.scalar.preload_act_table_set(EXP_LN)
            act.wait_ge(s["ld_w"], 16 * n_loads[0])
            nc.scalar.activation(aneg[:, :, :], aneg[:, :, :], ACT.Exp).then_inc(s["setup_a"], 1)
            act.wait_ge(s["setup_v"], 3)

            def ln_scale(kind, b):
                st, i = ln_set(kind, b)
                w = LN[st][0]
                act.wait_ge(s["mv_" + st], i + 1)
                nc.scalar.activation(lnv[:, w, :], mv[:, w, :, 1], ACT.Ln, bias=col(EPS_LN)).then_inc(s["lnv_" + st], 1)
                act.wait_ge(s["lnv_" + st], i + 1)
                nc.scalar.activation(rstd[:, w, :], lnv[:, w, :], ACT.Exp, scale=-0.5).then_inc(s["rstd_" + st], 1)

            def ln_high(kind, b):
                st, i = ln_set(kind, b)
                _, _, xt, (bank, _) = LN[st]
                act.wait_ge(s["xt_" + st], i + 1)
                nc.scalar.activation(xt[:, 0, :, :], ps[:, bank:bank + 2, :], ACT.Copy).then_inc(s["hi_" + st], 1)

            def hidden_chunk(which, i, f):
                hid, h_hi, _ = HIDDEN[which]
                bank = (None, 4, 0)[which] + f % 2
                act.wait_ge(s[f"up{which}"], i * FC + f + 1)
                if f >= 4:
                    act.wait_ge(s[f"hlo{which}"], i * FC + f - 3)
                nc.scalar.activation(hid[:, f % 4, :], ps[:, bank, :], ACT.Relu,
                                     bias=b1[:, f:f + 1], scale=col(S_H)).then_inc(s[f"hid{which}"], 1)
                nc.scalar.activation(h_hi[:, f, :], ps[:, bank, :], ACT.Relu,
                                     bias=b1[:, f:f + 1], scale=col(S_H)).then_inc(s[f"hhi{which}"], 1)

            def qkv_out(b):
                q4 = qk.rearrange("p (a b) n -> p a b n", a=2)
                s4 = sq.rearrange("p (a b n) -> p a b n", a=2, b=TT)
                for tt in range(TT):
                    act.wait_ge(s["qkv"], b * TT + tt + 1)
                    pq = ps[:, QKV_BANK[tt], :].rearrange("p (a n) -> p a n", a=2)
                    nc.scalar.activation(q4[:, :, tt, :], pq, ACT.Copy, scale=col(A_QKV)).then_inc(s["qkev"], 1)
                    nc.scalar.activation(s4[:, :, tt, :], pq, ACT.Square, scale=col(A_QKV)).then_inc(s["msq_sq"], 1)

            def rms_scale(b):
                act.wait_ge(s["msq_red"], b + 1)
                nc.scalar.activation(msq[:, :], msq[:, :], ACT.Ln, bias=col(EPS_RMS), scale=1.0 / HD).then_inc(s["msq_ln"], 1)
                act.wait_ge(s["msq_ln"], b + 1)
                nc.scalar.activation(rms[:, :], msq[:, :], ACT.Exp, scale=-0.5).then_inc(s["msq_rs"], 1)

            def qk_high(b):
                act.wait_ge(s["roped"], b + 1)
                for a in range(2):
                    step = 2 - a
                    src = rot[:, a * TT * DIM:(a + 1) * TT * DIM].rearrange("p (h d) -> p h d", d=HD)
                    for c in range(2):
                        o = c * step * HD
                        nc.scalar.activation(qka[:, a, :, o:o + HD], src, ACT.Copy).then_inc(s["qhi"], 1)
                for j in range(0, 8, 2):
                    act.wait_ge(s["qktp"], b * 8 + j + 1)
                    nc.scalar.activation(*qk_evac(j), ACT.Copy).then_inc(s["qkta"], 1)

            def pre(b):
                ln_scale("attn", b)
                ln_high("attn", b)
                qkv_out(b)
                rms_scale(b)
                qk_high(b)

            def body(b, has_a, has_m, has_next):
                def decays(n):
                    m = b - 1
                    if n == 0:
                        act.wait_ge(s["delta"], b * DT)
                    if n >= 2:
                        act.wait_ge(s["scan"], m * NS + n - 1)
                    for d in range(DT):
                        ins = nc.scalar.activation(decay[:, n % 2, d, 1:SEQ], delta[:, d, 1:SEQ], ACT.Exp,
                                                   scale=aneg[:, d, n:n + 1])
                    ins.then_inc(s["decay"], 1)

                def numerators(i):
                    act.wait_ge(s["score"], b * UNITS + i + 1)
                    if i >= PSLOTS:
                        act.wait_ge(s["pv"], b * PVS + (i - PSLOTS) // GROUP + 1)
                    bank = 2 * (i % 2)
                    nc.scalar.activation(prob[:, i % PSLOTS, :, :], ps[:, bank:bank + 2, :], ACT.Exp,
                                         scale=col(LOGIT)).then_inc(s["prob"], 1)

                if has_m:
                    decays(0)
                for n in range(NS):
                    if has_m and n + 1 < NS:
                        decays(n + 1)
                    if has_a:
                        numerators(2 * n)
                        numerators(2 * n + 1)
                if has_a:
                    act.wait_ge(s["ontp"], b + 1)
                    nc.scalar.activation(oc, ps[:, 4:6, :], ACT.Copy).then_inc(s["ocev"], 1)
                    ln_scale("ffn1", b)
                if has_m:
                    ln_scale("ffn2", b)
                if has_a:
                    ln_high("ffn1", b)
                if has_m:
                    ln_high("ffn2", b)
                if has_a:
                    for f in range(FC):
                        hidden_chunk(1, b, f)
                for f in range(FC):
                    if has_a and f == 4:
                        ln_scale("scan", b)
                    if has_next and f == 6:
                        ln_scale("attn", b + 1)
                    if has_m:
                        hidden_chunk(2, b - 1, f)
                if has_a:
                    ln_high("scan", b)
                if has_next:
                    ln_high("attn", b + 1)
                if has_a:
                    act.wait_ge(s["xdp"], b + 1)
                    if has_m:
                        act.wait_ge(s["bstore"], 16 * b)
                    nc.scalar.activation(xdbl[:, :], ps[0:XD, WX_BANK, :], ACT.Copy, scale=sc[0:XD, A_X:A_X + 1]).then_inc(s["xdev"], 1)
                if has_next:
                    qkv_out(b + 1)
                if has_a:
                    for d in range(DT):
                        act.wait_ge(s["res"], b * DT + d + 1)
                        nc.scalar.activation(sres[:, d, :], ps[:, RES_BANK[d], :], ACT.Copy, scale=col(A_IN)).then_inc(s["rescp"], 1)
                if has_next:
                    rms_scale(b + 1)
                if has_a:
                    for d in range(DT):
                        act.wait_ge(s["zc"], b * DT + d + 1)
                        nc.scalar.activation(hst[:, 1, d, :], hst[:, 1, d, :], ACT.Exp).then_inc(s["ez"], 1)
                    for d in range(DT):
                        act.wait_ge(s["ez"], b * DT + d + 1)
                        nc.scalar.activation(hst[:, 1, d, :], hst[:, 1, d, :], ACT.Ln, bias=1.0).then_inc(s["lz"], 1)
                    for d in range(DT):
                        act.wait_ge(s["conv"], b * DT + d + 1)
                        nc.scalar.activation(u[:, d, :], hst[:, 0, d, :], ACT.Silu, bias=bconv[:, d:d + 1]).then_inc(s["uu"], 1)
                    act.wait_ge(s["rescp"], (b + 1) * DT)
                    nc.scalar.activation(sres[:, :, :], sres[:, :, :], ACT.Silu).then_inc(s["sres_"], 1)
                    nc.scalar.preload_act_table_set(EXP_LN)
                if has_next:
                    qk_high(b + 1)

            iterations(act, pre, body)

        @block.vector
        def _(dve):
            v = nc.vector
            dve.wait_ge(s["ld_w"], 16 * n_loads[0])
            dve.wait_ge(s["setup_p"], 7)
            k = [0]

            def link(ins):
                k[0] += 1
                ins.then_inc(s["setup_ev"], 1)
                dve.wait_ge(s["setup_ev"], k[0])

            for i, src, op in ((A_QKV, ldq, ALU.max), (A_IN, ldi, ALU.max), (A_X, ldx, ALU.max),
                               (G1, ldw1, ALU.add), (G2, ldw2, ALU.add)):
                v.tensor_reduce(col(i), src, AX.XY, op, apply_absolute_value=True)
            v.tensor_reduce(col(MQ), qsc[:, 0, 0, :], AX.X, ALU.max, apply_absolute_value=True)
            v.tensor_reduce(col(MK), qsc[:, 1, 0, :], AX.X, ALU.max, apply_absolute_value=True)
            v.memset(col(EPS_LN), LN_EPS)
            v.memset(col(EPS_RMS), RMS_EPS)
            v.tensor_reduce(col(MB), b1[:, :], AX.X, ALU.max, apply_absolute_value=True).then_inc(s["setup_v"], 1)
            dve.wait_ge(s["setup_p"], 4)
            dve.wait_ge(s["setup_r"], 1)
            link(v.tensor_reduce(red[:, 0:1], ps[0:8, 0, 0:P], AX.X, ALU.max))
            link(v.tensor_reduce(red[:, 1:2], ps[0:8, 0, 0:P], AX.X, ALU.add))
            link(v.tensor_scalar(reddiag[:, 0:8], identf[0:8, 0:8], red[:, 0:1], None, ALU.mult))
            v.tensor_scalar(reddiag[:, 8:16], identf[0:8, 0:8], red[:, 1:2], None, ALU.mult).then_inc(s["setup_v"], 1)
            dve.wait_ge(s["setup_r"], 2)
            link(v.tensor_copy(col(0, 3), ps[:, 1, 0:3]))
            link(v.tensor_copy(col(G1, 2), ps[:, 1, 8 + G1:8 + G1 + 2]))
            link(v.tensor_copy(col(MB), ps[:, 1, MB:MB + 1]))
            link(v.tensor_scalar(col(A_QKV, 3), col(A_QKV, 3), 1e-30, None, ALU.max))
            link(v.tensor_scalar(col(MQ, 2), col(MQ, 2), 1e-30, None, ALU.max))
            link(v.reciprocal(col(I_QKV, 3), col(A_QKV, 3)))
            link(v.reciprocal(col(IQ, 2), col(MQ, 2)))
            link(v.tensor_tensor(col(TMP), col(MQ), col(MK), ALU.mult))
            link(v.tensor_scalar(col(LOGIT), col(TMP), float(HD) ** -0.5, None, ALU.mult))
            link(v.tensor_scalar(big_logits[:, :], col(LOGIT), MAX_LOGIT_UNSHIFTED / HD, None, ALU.is_gt))
            link(v.tensor_scalar(col(TH1, 2), col(G1, 2), 1.0 / (FF * DIM), Q_EPS, ALU.mult, ALU.add))
            link(v.tensor_scalar(col(NTH1, 2), col(TH1, 2), -0.5, None, ALU.mult))
            link(v.tensor_scalar(col(TH1, 2), col(TH1, 2), 0.5, None, ALU.mult))
            link(v.tensor_scalar(col(INV_S), col(MB), 1.0 / LN_BOUND, 1.0, ALU.mult, ALU.add))
            link(v.reciprocal(col(S_H), col(INV_S)))
            link(v.tensor_scalar(b1[:, :], b1[:, :], col(S_H), None, ALU.mult))
            for i, src, hi_, lo_ in ((I_QKV, ldq, wqkv_hi, wqkv_lo), (I_IN, ldi, win_hi, win_lo), (I_X, ldx, wx_hi, wx_lo)):
                n = src.shape[1] * src.shape[2]
                link(v.tensor_scalar(src, src, col(i), None, ALU.mult))
                link(v.tensor_copy(hi_[:, :, :], src))
                link(v.tensor_tensor(lo_[:, :, :], src, hi_[:, :, :], ALU.subtract))
            for thr, nthr, src, dst in ((TH1, NTH1, ldw1, tern1), (TH2, NTH2, ldw2, tern2)):
                tmp = stmp.rearrange("p (f n) -> p f n", f=src.shape[1])
                link(v.tensor_scalar(tmp, src, col(nthr), None, ALU.is_lt))
                link(v.scalar_tensor_tensor(dst, src, col(thr), tmp, ALU.is_gt, ALU.subtract))
            for a in range(2):
                for tab, w in ((ropec, 0), (ropes, 1)):
                    link(v.tensor_scalar(qsc[:, a, w, :], qsc[:, a, w, :], col(IQ + a), None, ALU.mult))
                    link(v.tensor_tensor(tab[:, a, :, :], tab[:, a, :, :],
                                         qsc[:, a, w, :].unsqueeze(1).to_broadcast([P, TT, HD]), ALU.mult))
            dve.wait_ge(s["setup_a"], 1)
            v.tensor_scalar(aneg[:, :, :], aneg[:, :, :], -1.0, None, ALU.mult).then_inc(s["setup_v"], 1)
            for f in range(8):
                dve.wait_ge(s["setup_t"], f + 1)
                if f < 4:
                    dst = w1t[:, f // 2, (f % 2) * 512:(f % 2) * 512 + 512]
                    v.tensor_copy(dst, psh[f][:, 0:512]).then_inc(s["setup_tev"], 1)
                else:
                    g = f - 4
                    v.tensor_copy(w2t[:, 2 * g:2 * g + 2, :],
                                  psh[f][:, 0:512].rearrange("p (a n) -> p a n", a=2)).then_inc(s["setup_tev"], 1)

            need_max = dve.value_load(big_logits[0:1, 0:1])

            def guard(b):
                n = HEADS * TT
                for j in range(n):
                    h, tt = j // TT, j % TT
                    dve.wait_ge(s["guard_s"], b * n + j + 1)
                    v.reduce_max(rowmax[:, tt * HEADS + h:tt * HEADS + h + 1], ps[:, j % 4, :], AX.X).then_inc(s["guard_m"], 1)
                dve.wait_ge(s["guard_m"], (b + 1) * n)
                v.tensor_scalar(qka[:, 0, :, SHIFT], rowmax[:, :], -1.0, None, ALU.mult).then_inc(s["guard_h"], 1)
                dve.wait_ge(s["guard_h"], b + 1)
                v.scalar_tensor_tensor(qka[:, 0, :, SHIFT + 1], rowmax[:, :], -1.0, qka[:, 0, :, SHIFT],
                                       ALU.mult, ALU.subtract).then_inc(s["guard_w"], 1)
                for j in range(4):
                    dve.wait_ge(s["guard_t"], b * 4 + j + 1)
                    v.tensor_copy(*qk_evac(j)).then_inc(s["guard_c"], 1)

            def ln_rows(kind, b, src):
                st, i = ln_set(kind, b)
                w, rows, _, _ = LN[st]
                for tt in range(TT):
                    ins = v.bn_stats(bnst[:, w, tt, :], src[:, tt, :])
                ins.then_inc(s["stats_" + st], 1)
                dve.wait_ge(s["stats_" + st], i + 1)
                stand_alone(dve)
                for tt in range(TT):
                    ins = v.bn_aggr(mv[:, w, tt, :], bnst[:, w, tt, :])
                ins.then_inc(s["mv_" + st], 1)
                dve.wait_ge(s["rstd_" + st], i + 1)
                for tt in range(TT):
                    ins = v.tensor_scalar(rows[:, tt, :], src[:, tt, :], mv[:, w, tt, 0:1], rstd[:, w, tt:tt + 1],
                                          ALU.subtract, ALU.mult)
                ins.then_inc(s["xn_" + st], 1)

            def ln_low(kind, b):
                st, i = ln_set(kind, b)
                _, _, xt, (bank, _) = LN[st]
                dve.wait_ge(s["hi_" + st], i + 1)
                v.tensor_tensor(xt[:, 1, :, :], ps[:, bank:bank + 2, :], xt[:, 0, :, :], ALU.subtract).then_inc(s["lo_" + st], 1)

            def hidden_low(which, i, f):
                hid, h_hi, h_lo = HIDDEN[which]
                dve.wait_ge(s[f"hhi{which}"], i * FC + f + 1)
                v.tensor_tensor(h_lo[:, f, :], hid[:, f % 4, :], h_hi[:, f, :], ALU.subtract).then_inc(s[f"hlo{which}"], 1)

            def ffn_out(which, i, src, dst, bias):
                dve.wait_ge(s[f"down{which}"], i + 1)
                dve.wait_ge(s[bias], i + 1)
                for tt in range(TT):
                    v.scalar_tensor_tensor(dst[:, tt, :], tile_bank((None, 6, 2)[which], tt), col(INV_S), src[:, tt, :],
                                           ALU.mult, ALU.add).then_inc(s[f"fout{which}"], 1)

            def scan_step(m, n):
                dve.wait_ge(s["decay"], m * NS + n + 1)
                dve.wait_ge(s["dbu"], m * NS + n + 1)
                flat = hst[:, n % HSLOTS, :, :].rearrange("p d t -> p (d t)")
                v.tensor_tensor_scan(flat, decay[:, n % 2, :, :].rearrange("p d t -> p (d t)"), flat, 0.0,
                                     ALU.mult, ALU.add).then_inc(s["scan"], 1)

            def acc_step(m, n):
                for tt in range(TT):
                    dve.wait_ge(s["htp"], (m * NS + n) * TT + tt + 1)
                    src = ps[:, 4 + tt % 2, :]
                    if n == 0:
                        ins = v.tensor_scalar(acc[:, tt, :], src, ctok[:, tt, n:n + 1], None, ALU.mult)
                    else:
                        ins = v.scalar_tensor_tensor(acc[:, tt, :], src, ctok[:, tt, n:n + 1], acc[:, tt, :],
                                                     ALU.mult, ALU.add)
                    ins.then_inc(s["accd"], 1)

            def group_out(b, g):
                dve.wait_ge(s["pv"], b * PVS + 2 * g + 2)
                if g >= 1:
                    dve.wait_ge(s["otp"], b * NG + g)
                v.tensor_copy(ot, ps[:, 6, :]).then_inc(s["oev"], 1)

            def group_norm(b, g):
                dve.wait_ge(s["otp"], b * NG + g + 1)
                o4 = ps[:, 7, :].rearrange("p (t j r) -> p t j r", t=TT, j=GROUP)
                v.reciprocal(rden[:, :, :], o4[:, :, :, HD]).then_inc(s["rden"], 1)
                dve.wait_ge(s["rden"], b * NG + g + 1)
                v.tensor_tensor(on[:, :, g * GROUP * HD:(g + 1) * GROUP * HD].rearrange("p t (j d) -> p t j d", j=GROUP),
                                o4[:, :, :, 0:HD], rden[:, :, :].unsqueeze(3).to_broadcast([P, TT, GROUP, HD]),
                                ALU.mult).then_inc(s["on"], 1)

            def values_out(b):
                for tt in range(TT):
                    dve.wait_ge(s["qkv_v"], b * TT + tt // 2 * 2 + 2)
                    v.tensor_scalar(vaug[:, tt, :, 0:HD], tile_bank(V_BANK[0], tt).rearrange("p (h d) -> p h d", d=HD),
                                    col(A_QKV), None, ALU.mult).then_inc(s["vev"], 1)

            def mean_squares(b):
                dve.wait_ge(s["msq_sq"], (b + 1) * TT)
                v.tensor_reduce(msq[:, :], sq.rearrange("p (a d) -> p a d", d=HD), AX.X, ALU.add).then_inc(s["msq_red"], 1)

            def rope(b):
                dve.wait_ge(s["qn"], b + 1)
                v.tensor_tensor(heads_view(sq), heads_view(qn),
                                ropec[:, :, :, :].rearrange("p a b d -> p (a b) d").unsqueeze(2)
                                .to_broadcast([P, 2 * TT, HEADS, HD]), ALU.mult).then_inc(s["ropea"], 1)
                dve.wait_ge(s["rot_s"], 2 * (b + 1))
                dve.wait_ge(s["ropea"], b + 1)
                v.tensor_tensor(rot, sq, rot, ALU.add).then_inc(s["roped"], 1)
                dve.wait_ge(s["roped"], b + 1)
                v.memset(qka[:, 0, :, SHIFT:ROWS], 0.0)
                v.memset(qka[:, 1, :, SHIFT:ROWS], 1.0)

            def qk_low(b):
                dve.wait_ge(s["qhi"], 4 * (b + 1))
                for a in range(2):
                    o = (1 + a) * HD
                    src = rot[:, a * TT * DIM:(a + 1) * TT * DIM].rearrange("p (h d) -> p h d", d=HD)
                    v.tensor_tensor(qka[:, a, :, o:o + HD], src, qka[:, a, :, 0:HD], ALU.subtract).then_inc(s["qlo"], 1)
                for j in range(1, 8, 2):
                    dve.wait_ge(s["qktp"], b * 8 + j + 1)
                    v.tensor_copy(*qk_evac(j)).then_inc(s["qktv"], 1)
                with dve.If(need_max == 1):
                    guard(b)
                with dve.Else():
                    dve.sem_inc(s["waited"], 1)

            def pre(b):
                dve.wait_ge(s["ld_x"], 16 * (b + 1))
                ln_rows("attn", b, xa)
                ln_low("attn", b)
                values_out(b)
                mean_squares(b)
                rope(b)
                qk_low(b)

            def conv_tile(b, d):
                dve.wait_ge(s["xin"], b * DT + d + 1)
                pad = xpad[:, d % 2, :]
                v.tensor_scalar(pad[:, 1:1 + SEQ], ps[:, X_BANK[d], :], col(A_IN), None, ALU.mult).then_inc(s["xpad"], 1)
                dve.wait_ge(s["xpad"], b * DT + d + 1)
                cv = hst[:, 0, d, :]
                taps = CONV - 1
                v.tensor_scalar(cv, pad[:, 0:SEQ], kconv[:, d, 0:1], None, ALU.mult).then_inc(s["conv1"], 1)
                for j in range(1, CONV):
                    dve.wait_ge(s["conv1"], (b * DT + d) * taps + j)
                    v.scalar_tensor_tensor(cv, pad[:, j:j + SEQ], kconv[:, d, j:j + 1], cv, ALU.mult,
                                           ALU.add).then_inc(s["conv1"] if j < taps else s["conv"], 1)

            def body(b, has_a, has_m, has_next):
                m = b - 1
                for n in range(NS + 1):
                    if has_m:
                        if n < NS:
                            scan_step(m, n)
                        if n >= 1:
                            acc_step(m, n - 1)
                    if has_a and n > GROUP and n % GROUP == 1:
                        group_norm(b, n // GROUP - 1)
                    if has_a and n >= GROUP and n % GROUP == 0:
                        group_out(b, n // GROUP - 1)
                if has_a:
                    group_norm(b, NG - 1)
                if has_m:
                    dve.wait_ge(s["sres_"], b)
                    for d in range(DT):
                        dve.wait_ge(s["ytp"], m * DT + d + 1)
                        v.scalar_tensor_tensor(ybuf[:, d, :], u[:, d, :], dskip[:, d:d + 1], ps[:, d, :],
                                               ALU.mult, ALU.add).then_inc(s["yskip"], 1)
                        dve.wait_ge(s["yskip"], m * DT + d + 1)
                        v.tensor_tensor(ybuf[:, d, :], ybuf[:, d, :], sres[:, d, :], ALU.mult).then_inc(s["y"], 1)
                if has_a:
                    dve.wait_ge(s["bias_proj"], b + 1)
                    for tt in range(TT):
                        dve.wait_ge(s["proj"], b * TT + tt // 2 * 2 + 2)
                        v.tensor_tensor(xa[:, tt, :], tile_bank(6, tt), xa[:, tt, :], ALU.add).then_inc(s["pjev"], 1)
                    dve.wait_ge(s["pjev"], (b + 1) * TT)
                    ln_rows("ffn1", b, xa)
                if has_m:
                    dve.wait_ge(s["bias_out"], b)
                    dve.wait_ge(s["store"], 16 * b)
                    for tt in range(TT):
                        dve.wait_ge(s["wo"], m * TT + tt // 2 * 2 + 2)
                        v.tensor_tensor(yo[:, tt, :], tile_bank(2, tt), xb[:, tt, :], ALU.add).then_inc(s["woev"], 1)
                    dve.wait_ge(s["woev"], b * TT)
                    ln_rows("ffn2", b, yo)
                if has_a:
                    ln_low("ffn1", b)
                if has_m:
                    ln_low("ffn2", b)
                if has_a:
                    for f in range(FC):
                        hidden_low(1, b, f)
                for f in range(FC):
                    if has_m:
                        hidden_low(2, m, f)
                    if has_a and f == 1:
                        ffn_out(1, b, xa, xb, "bias_f1")
                    if has_a and f == 2:
                        dve.wait_ge(s["fout1"], (b + 1) * TT)
                        ln_rows("scan", b, xb)
                    if has_next and f == 4:
                        dve.wait_ge(s["ld_x"], 16 * (b + 2))
                        ln_rows("attn", b + 1, xa)
                if has_m:
                    ffn_out(2, m, yo, yo, "bias_f2")
                if has_a:
                    ln_low("scan", b)
                if has_next:
                    ln_low("attn", b + 1)
                if has_a:
                    v.memset(xpad[:, :, 0:1], 0.0)
                    v.memset(xpad[:, :, 1 + SEQ:SEQ + CONV - 1], 0.0)
                    for d in range(DT):
                        conv_tile(b, d)
                if has_next:
                    values_out(b + 1)
                    mean_squares(b + 1)
                if has_a:
                    dve.wait_ge(s["ctp"], b + 1)
                    v.tensor_copy(ctok[:, :, :], ps[:, C_BANK, :].rearrange("p (t r) -> p t r", t=TT)[:, :, RANK + NS:XD]).then_inc(s["cev"], 1)
                    for d in range(DT):
                        dve.wait_ge(s["dtp"], b * DT + d + 1)
                        v.tensor_scalar(hst[:, 1, d, :], ps[:, DT_BANK[d], :], bdt[:, d:d + 1], 30.0, ALU.add, ALU.min).then_inc(s["zc"], 1)
                    for d in range(DT):
                        dve.wait_ge(s["lz"], b * DT + d + 1)
                        v.scalar_tensor_tensor(delta[:, d, :], ps[:, DT_BANK[d], :], bdt[:, d:d + 1], hst[:, 1, d, :],
                                               ALU.add, ALU.max).then_inc(s["delta"], 1)
                if has_next:
                    rope(b + 1)
                    qk_low(b + 1)

            iterations(dve, pre, body)

        @block.tensor
        def _(pe):
            mm, tp = nc.tensor.matmul, nc.tensor.transpose
            pe.wait_ge(s["setup_p"], 7)
            pe.wait_ge(s["setup_v"], 1)
            tp(ps[0:8, 0, 0:P], sc[:, 0:8], identf[:, :]).then_inc(s["setup_r"], 1)
            pe.wait_ge(s["setup_v"], 2)
            mm(ps[:, 1, 0:16], ones8[:, :], reddiag[:, :], start=True, stop=True).then_inc(s["setup_r"], 1)
            pe.wait_ge(s["setup_v"], 3)
            for f in range(4):
                c, base = f // 2, (f % 2) * 4
                for i in range(4):
                    ins = tp(psh[f][:, i * P:(i + 1) * P], tern1[:, base + i, c * P:(c + 1) * P], identh[:, :])
                ins.then_inc(s["setup_t"], 1)
            for g in range(4):
                for i in range(4):
                    ins = tp(psh[4 + g][:, i * P:(i + 1) * P],
                             tern2[:, i % 2, (2 * g + i // 2) * P:(2 * g + i // 2 + 1) * P], identh[:, :])
                ins.then_inc(s["setup_t"], 1)
            pe.wait_ge(s["setup_tev"], 8)

            need_max = pe.value_load(big_logits[0:1, 0:1])

            def q_or_k_transposes(j):
                bank = QK_BANK[j]
                for e in range(2):
                    hp = (j % 4) * 2 + e
                    for tt in range(TT):
                        o = e * SEQ + tt * P
                        src = qka[:, j // 4, tt * HEADS + 2 * hp:tt * HEADS + 2 * hp + 2, :].rearrange("p h r -> p (h r)")
                        ins = tp(psh[bank][:, o:o + P], src, identh[:, :])
                return ins

            def guard(b):
                n = HEADS * TT
                for j in range(n):
                    h, tt = j // TT, j % TT
                    r, hp = (h % 2) * ROWS, h // 2
                    if j >= 4:
                        pe.wait_ge(s["guard_m"], b * n + j - 3)
                    mm(ps[:, j % 4, :], qt[r:r + ROWS, hp, tt * P:(tt + 1) * P], kt[r:r + ROWS, hp, :],
                       start=True, stop=True).then_inc(s["guard_s"], 1)
                pe.wait_ge(s["guard_w"], b + 1)
                for j in range(4):
                    q_or_k_transposes(j).then_inc(s["guard_t"], 1)
                pe.wait_ge(s["guard_c"], 4 * (b + 1))

            def ln_transposes(kind, b):
                st, i = ln_set(kind, b)
                _, rows, _, banks = LN[st]
                pe.wait_ge(s["xn_" + st], i + 1)
                for c in range(KC):
                    for tt in range(TT):
                        ins = tp(ps[:, banks[c], tt * P:(tt + 1) * P], rows[:, tt, c * P:(c + 1) * P], identf[:, :])
                ins.then_inc(s["xt_" + st], 1)

            def ln_done(kind, b):
                st, i = ln_set(kind, b)
                pe.wait_ge(s["lo_" + st], i + 1)

            def ffn(which, i, kind, b):
                xt = LN[ln_set(kind, b)[0]][2]
                _, h_hi, h_lo = HIDDEN[which]
                up_bank, out_bank = (None, (4, 6), (0, 2))[which]
                ln_done(kind, b)

                def up(f):
                    if f >= 2:
                        pe.wait_ge(s[f"hhi{which}"], i * FC + f - 1)
                    for c in range(KC):
                        for part in range(2):
                            ins = mm(ps[:, up_bank + f % 2, :], w1t[:, c, f * P:(f + 1) * P], xt[:, part, c, :],
                                     start=(c + part == 0), stop=(c + part == KC))
                    ins.then_inc(s[f"up{which}"], 1)

                def down(f):
                    pe.wait_ge(s[f"hlo{which}"], i * FC + f + 1)
                    for tt in range(TT):
                        for part, h in enumerate((h_hi, h_lo)):
                            ins = mm(tile_bank(out_bank, tt), h[:, f, tt * P:(tt + 1) * P], w2t[:, f, :],
                                     start=(f == 0 and part == 0 and tt % 2 == 0),
                                     stop=(f == FC - 1 and part == 1 and tt % 2 == 1), skip_group_check=True)
                    return ins

                for f in range(FC + 2):
                    if f < FC:
                        up(f)
                    if f >= 2:
                        ins = down(f - 2)
                ins.then_inc(s[f"down{which}"], 1)

            def split_mm(dst, xt, w_hi, w_lo, w_is_lhs, xs, ws):
                n = 0
                for c in range(KC):
                    for part, wp in ((0, w_hi), (0, w_lo), (1, w_hi)):
                        xo, wo_ = xt[:, part, c, xs], wp[:, c, ws]
                        a, bb = (wo_, xo) if w_is_lhs else (xo, wo_)
                        ins = mm(dst, a, bb, start=(n == 0), stop=(n == 3 * KC - 1))
                        n += 1
                return ins

            def qkv(b):
                ln_done("attn", b)
                for tt in range(TT):
                    split_mm(tile_bank(V_BANK[0], tt), xt_a, wqkv_hi, wqkv_lo, False, slice(tt * P, (tt + 1) * P),
                             slice(2 * DIM, 3 * DIM)).then_inc(s["qkv_v"], 1)
                for tt in range(TT):
                    if tt >= 2:
                        pe.wait_ge(s["vev"], b * TT + 2 * (tt - 1))
                    split_mm(ps[:, QKV_BANK[tt], :], xt_a, wqkv_hi, wqkv_lo, False, slice(tt * P, (tt + 1) * P),
                             slice(0, 2 * DIM)).then_inc(s["qkv"], 1)

            def qk_transposes(b):
                pe.wait_ge(s["qlo"], 2 * (b + 1))
                for j in range(8):
                    if j >= 4:
                        pe.wait_ge(s["qkta"] if j % 2 == 0 else s["qktv"], b * 4 + (j - 4) // 2 + 1)
                    q_or_k_transposes(j).then_inc(s["qktp"], 1)
                pe.wait_ge(s["qkta"], 4 * (b + 1))
                pe.wait_ge(s["qktv"], 4 * (b + 1))
                with pe.If(need_max == 1):
                    guard(b)
                with pe.Else():
                    pe.sem_inc(s["waited"], 1)

            def pre(b):
                ln_transposes("attn", b)
                qkv(b)
                qk_transposes(b)

            def body(b, has_a, has_m, has_next):
                m = b - 1

                def scores(i):
                    h, k0 = unit(i)
                    r, hp = (h % 2) * ROWS, h // 2
                    if i >= 2:
                        pe.wait_ge(s["prob"], b * UNITS + i - 1)
                    for kk in range(2):
                        ins = mm(ps[:, 2 * (i % 2) + kk, :], kt[r:r + ROWS, hp, (k0 + kk) * P:(k0 + kk + 1) * P],
                                 qt[r:r + ROWS, hp, :], start=True, stop=True)
                    ins.then_inc(s["score"], 1)

                def values(k):
                    g, pair = k // 2, k % 2
                    pe.wait_ge(s["prob"], b * UNITS + GROUP * (k + 1))
                    if pair == 0 and g >= 1:
                        pe.wait_ge(s["oev"], b * NG + g)
                    for kk in range(2):
                        for j in range(GROUP):
                            kc = 2 * pair + kk
                            ins = mm(ps[32 * j:32 * j + 32, 6, :], vaug[:, kc, g * GROUP + j, :],
                                     prob[:, (k * GROUP + j) % PSLOTS, kk, :], start=(kc == 0), stop=(kc == TT - 1))
                    ins.then_inc(s["pv"], 1)

                def out_rows(g):
                    pe.wait_ge(s["oev"], b * NG + g + 1)
                    if g >= 1:
                        pe.wait_ge(s["on"], b * NG + g)
                    for tt in range(TT):
                        ins = tp(ps[:, 7, tt * P:(tt + 1) * P], ot[:, tt * P:(tt + 1) * P], identf[:, :])
                    ins.then_inc(s["otp"], 1)

                def states(n, tiles):
                    if n == 0:
                        pe.wait_ge(s["delta"], b * DT)
                        pe.wait_ge(s["cev"], b)
                    pe.wait_ge(s["scan"], m * NS + n + 1)
                    for tt in tiles:
                        if n * TT + tt >= 2:
                            pe.wait_ge(s["accd"], (m * NS + n) * TT + tt - 1)
                        for d in range(DT):
                            ins = tp(ps[:, 4 + tt % 2, d * P:(d + 1) * P], hst[:, n % HSLOTS, d, tt * P:(tt + 1) * P], identf[:, :])
                        ins.then_inc(s["htp"], 1)

                for n in range(NS + 1):
                    if has_a and n < NS:
                        scores(2 * n)
                    if has_m and n < NS:
                        states(n, (0, 1))
                    if has_a and n < NS:
                        scores(2 * n + 1)
                    if has_a and n >= 2 and n % 2 == 0:
                        values(n // 2 - 1)
                    if has_m and n < NS:
                        states(n, (2, 3))
                    if has_a and n >= GROUP and n % GROUP == 0:
                        out_rows(n // GROUP - 1)
                if has_m:
                    pe.wait_ge(s["accd"], b * NS * TT)
                    for d in range(DT):
                        for tt in range(TT):
                            ins = tp(ps[:, d, tt * P:(tt + 1) * P], acc[:, tt, d * P:(d + 1) * P], identf[:, :])
                        ins.then_inc(s["ytp"], 1)
                if has_a:
                    pe.wait_ge(s["on"], (b + 1) * NG)
                    for c in range(KC):
                        for tt in range(TT):
                            ins = tp(ps[:, 4 + c, tt * P:(tt + 1) * P], on[:, tt, c * P:(c + 1) * P], identf[:, :])
                    ins.then_inc(s["ontp"], 1)
                    pe.wait_ge(s["ocev"], b + 1)
                    for tt in range(TT):
                        for c in range(KC):
                            ins = mm(tile_bank(6, tt), oc[:, c, tt * P:(tt + 1) * P], wproj[:, c, :],
                                     start=(c == 0), stop=(c == KC - 1))
                        ins.then_inc(s["proj"], 1)
                if has_m:
                    pe.wait_ge(s["y"], b * DT)
                    for tt in range(TT):
                        for d in range(DT):
                            ins = mm(tile_bank(2, tt), ybuf[:, d, tt * P:(tt + 1) * P], wout[:, d, :],
                                     start=(d == 0), stop=(d == DT - 1))
                        ins.then_inc(s["wo"], 1)
                if has_a:
                    ln_transposes("ffn1", b)
                if has_m:
                    ln_transposes("ffn2", b)
                if has_a:
                    ffn(1, b, "ffn1", b)
                if has_m:
                    ffn(2, m, "ffn2", b)
                if has_a:
                    ln_transposes("scan", b)
                if has_next:
                    ln_transposes("attn", b + 1)
                if has_a:
                    ln_done("scan", b)
                    every = slice(0, SEQ)
                    split_mm(ps[0:XD, WX_BANK, :], xt_b, wx_hi, wx_lo, True, every, slice(0, XD)).then_inc(s["xdp"], 1)
                    for d in range(DT):
                        if X_BANK[d] == WX_BANK:
                            pe.wait_ge(s["xdev"], b + 1)
                        split_mm(ps[:, X_BANK[d], :], xt_b, win_hi, win_lo, True, every,
                                 slice(d * P, (d + 1) * P)).then_inc(s["xin"], 1)
                if has_next:
                    if has_m:
                        pe.wait_ge(s["fout2"], b * TT)
                    qkv(b + 1)
                if has_a:
                    for d in range(DT):
                        pe.wait_ge(s["xpad"], b * DT + d + 1)
                        split_mm(ps[:, RES_BANK[d], :], xt_b, win_hi, win_lo, True, every,
                                 slice(D_INNER + d * P, D_INNER + (d + 1) * P)).then_inc(s["res"], 1)
                    pe.wait_ge(s["rescp"], b * DT + 1)
                    for tt in range(TT):
                        ins = tp(ps[:, C_BANK, tt * P:tt * P + XD], xdbl[:, tt * P:(tt + 1) * P], identf[0:XD, 0:XD])
                    ins.then_inc(s["ctp"], 1)
                    for d in range(DT):
                        if d < DT - 1:
                            pe.wait_ge(s["rescp"], b * DT + d + 2)
                        else:
                            pe.wait_ge(s["cev"], b + 1)
                        mm(ps[:, DT_BANK[d], :], wdt[:, d * P:(d + 1) * P], xdbl[0:RANK, :], start=True,
                           stop=True).then_inc(s["dtp"], 1)
                if has_next:
                    qk_transposes(b + 1)

            iterations(pe, pre, body)


_INS = ['L0_attn_a_x', 'L0_attn_a_w_qkv', 'L0_attn_a_q_scale', 'L0_attn_a_k_scale', 'L0_attn_a_w_proj',
        'L0_attn_a_b_proj', 'L0_attn_b_W_in', 'L0_attn_b_K_conv', 'L0_attn_b_b_conv', 'L0_attn_b_W_x',
        'L0_attn_b_W_dt', 'L0_attn_b_b_dt', 'L0_attn_b_A_log', 'L0_attn_b_D', 'L0_attn_b_W_out',
        'L0_attn_b_b_out', 'L0_ffn_W1', 'L0_ffn_b1', 'L0_ffn_W2', 'L0_ffn_b2']


def rope_tables():
    import numpy as _np
    freqs = (1.0 / _np.float32(2500) ** (_np.arange(HALF, dtype=_np.float32) / HALF)).astype(_np.float32)
    angle = _np.outer(_np.arange(SEQ, dtype=_np.float32), freqs).astype(_np.float32).astype(_np.float64)
    cos, sin = _np.cos(angle), _np.sin(angle)
    return (_np.concatenate([cos, cos], 1).astype(_np.float32), _np.concatenate([-sin, sin], 1).astype(_np.float32))


def kernel(**inputs):
    import numpy as _np
    import concourse.bacc as _bacc
    from concourse.bass_utils import run_bass_kernel_spmd as _run

    nc = _bacc.Bacc("TRN2", target_bir_lowering=False, num_devices=1)
    arrays, aps = {}, {}
    for name in _INS:
        a = _np.ascontiguousarray(inputs[name])
        arrays["in_" + name] = a
        aps[name] = nc.dram_tensor("in_" + name, a.shape, mybir.dt.from_np(a.dtype), kind="ExternalInput").ap()
    tables = []
    for name, a in zip(("rope_cos", "rope_sin"), rope_tables()):
        arrays[name] = a
        tables.append(nc.dram_tensor(name, a.shape, mybir.dt.from_np(a.dtype), kind="ExternalInput").ap())
    bt = nc.dram_tensor("b_rows", (NS, SEQ), FP32, kind="Internal").ap()
    out = nc.dram_tensor("out_0", (BATCH, SEQ, DIM), FP32, kind="ExternalOutput").ap()
    hybrid_block(nc, aps, out, tables[0], tables[1], bt)
    r = _run(nc, [arrays], core_ids=[0])
    return r.results[0]["out_0"]
```

```python
import numpy as np
import concourse.bass as bass
from concourse import mybir
from contextlib import ExitStack

FP32 = mybir.dt.float32
FP16 = mybir.dt.float16
ALU = mybir.AluOpType
ACT = mybir.ActivationFunctionType
AX = mybir.AxisListType

BATCH, SEQ, DIM = 8, 512, 256
P = 128
TT = SEQ // P
KC = DIM // P
HEADS = 16
HD = DIM // HEADS
HALF = HD // 2
ROWS = 64
D_INNER = 512
DT = D_INNER // P
NS = 16
RANK = 64
XD = RANK + 2 * NS
FF = 1024
FC = FF // P
CONV = 4
PAD = (CONV - 1) // 2
LN_EPS = 1e-5
RMS_EPS = 1e-6
EXP_LN = "natural_log_exp_and_others"
Q_EPS = 1e-5
SHIFT = 3 * HD
GROUP = 4
PSLOTS = 8
ROPE_AT, QK_HIGH_AT = 4, 6
LAG = 2
HSLOTS = 3
LN_BOUND = 256.0
MAX_LOGIT_UNSHIFTED = 60.0


def hybrid_block(nc, t, out, cos_t, sin_t, bt_scratch):
    x_d, y_d = t["L0_attn_a_x"], out

    with ExitStack() as ctx:
        def sb(name, shape, dt=FP32):
            return ctx.enter_context(nc.sbuf_tensor(name, shape, dt))

        def sem(name):
            return ctx.enter_context(nc.semaphore(name))

        wqkv_hi = sb("wqkv_hi", [P, KC, 3 * DIM], FP16)
        wqkv_lo = sb("wqkv_lo", [P, KC, 3 * DIM], FP16)
        win_hi = sb("win_hi", [P, KC, 2 * D_INNER], FP16)
        win_lo = sb("win_lo", [P, KC, 2 * D_INNER], FP16)
        wx_hi = sb("wx_hi", [P, KC, XD], FP16)
        wx_lo = sb("wx_lo", [P, KC, XD], FP16)
        wdt = sb("wdt", [RANK, D_INNER])
        wproj = sb("wproj", [P, KC, DIM])
        wout = sb("wout", [P, DT, DIM])
        w1t = sb("w1t", [P, KC, FF], FP16)
        w2t = sb("w2t", [P, FC, DIM], FP16)
        bproj = sb("bproj", [P, DIM])
        bout = sb("bout", [P, DIM])
        b2 = sb("b2", [P, DIM])
        b1 = sb("b1", [P, FC])
        bdt = sb("bdt", [P, DT])
        bconv = sb("bconv", [P, DT])
        dskip = sb("dskip", [P, DT])
        kconv = sb("kconv", [P, DT, CONV])
        kmid = sb("kmid", [P, DT])
        aneg = sb("aneg", [P, DT, NS])
        ropec = sb("ropec", [P, 2, TT, HD])
        ropes = sb("ropes", [P, 2, TT, HD])
        identf = sb("identf", [P, P])
        identh = sb("identh", [P, P], FP16)
        sc = sb("sc", [P, 32])
        big_logits = sb("big_logits", [P, 1], mybir.dt.uint32)
        rowmax = sb("rowmax", [P, TT * HEADS])
        ones8 = sb("ones8", [8, P])
        red = sb("red", [8, 2])
        reddiag = sb("reddiag", [8, 16])
        xa = sb("xa", [P, TT, DIM])
        xb = sb("xb", [P, TT, DIM])
        yo = sb("yo", [P, TT, DIM])
        xn = sb("xn", [P, TT, DIM])
        bnst = sb("bnst", [P, 2, TT, 6])
        mv = sb("mv", [P, 2, TT, 2])
        lnv = sb("lnv", [P, 2, TT])
        rstd = sb("rstd", [P, 2, TT])
        xt_a = sb("xt_a", [P, 2, KC, SEQ], FP16)
        qt = sb("qt", [P, HEADS // 2, SEQ], FP16)
        kt = sb("kt", [P, HEADS // 2, SEQ], FP16)
        vaug = sb("vaug", [P, TT, HEADS, 2 * HD])
        ot = xn[:, 0:2, :].rearrange("p a n -> p (a n)")
        rden = sb("rden", [P, TT, GROUP])
        on = sb("on", [P, TT, DIM])
        msq = sb("msq", [P, 2 * TT * HEADS])
        rms = sb("rms", [P, 2 * TT * HEADS])
        delta = sb("delta", [P, DT, SEQ])
        u = sb("u", [P, DT, SEQ])
        du = sb("du", [P, DT, SEQ])
        sres = sb("sres", [P, DT, SEQ])
        xdbl = sb("xdbl", [XD, SEQ])
        ctok = sb("ctok", [P, TT, NS])
        acc = sb("acc", [P, TT, D_INNER])
        decay = sb("decay", [P, 2, DT, SEQ])
        hst = sb("hst", [P, HSLOTS, DT, SEQ])
        bbc = sb("bbc", [P, 2, SEQ])
        ybuf = delta
        xs = acc
        zs = du
        arena = sb("arena", [P, PSLOTS * 2 * SEQ])
        prob = arena[:, :].rearrange("p (s k q) -> p s k q", s=PSLOTS, k=2)
        W = TT * SEQ
        qk = arena[:, 0:W].rearrange("p (a n) -> p a n", a=2 * TT)
        sq = arena[:, W:2 * W]
        qn = arena[:, 2 * W:3 * W]
        rot = arena[:, 3 * W:4 * W]
        qka = arena[:, 0:2 * W].bitcast(FP16).rearrange("p (a h r) -> p a h r", h=TT * HEADS, r=ROWS)
        hstf = hst[:, :, :, :].rearrange("p s d t -> p (s d t)")
        hid = hstf[:, 0:W].rearrange("p (s n) -> p s n", s=4)
        h_hi = hstf[:, W:2 * W].bitcast(FP16).rearrange("p (f n) -> p f n", f=FC)
        h_lo = hstf[:, 2 * W:3 * W].bitcast(FP16).rearrange("p (f n) -> p f n", f=FC)
        oc = hstf[:, 2 * W:2 * W + KC * SEQ].rearrange("p (c n) -> p c n", c=KC)
        xt_b = qt[:, 0:4, :].rearrange("p (h c) n -> p h c n", h=2)
        LN = {"a": (0, xn, xt_a, (0, 1)), "b": (1, on, xt_b, (4, 5))}
        ldq = arena[:, 0:KC * 3 * DIM].rearrange("p (c n) -> p c n", c=KC)
        ldi = arena[:, 1536:1536 + KC * 2 * D_INNER].rearrange("p (c n) -> p c n", c=KC)
        ldx = arena[:, 3584:3584 + KC * XD].rearrange("p (c n) -> p c n", c=KC)
        ldw1 = sres[:, :, :].rearrange("p a n -> p (a n)").rearrange("p (f n) -> p f n", f=FC)
        ldw2 = u[:, :, :].rearrange("p a n -> p (a n)").rearrange("p (c n) -> p c n", c=KC)
        accf = acc[:, :, :].rearrange("p a n -> p (a n)")
        tern1 = accf[:, 0:1024].bitcast(FP16).rearrange("p (f n) -> p f n", f=FC)
        tern2 = accf[:, 1024:2048].bitcast(FP16).rearrange("p (c n) -> p c n", c=KC)
        stmp = du[:, :, :].rearrange("p a n -> p (a n)")
        qsc = sb("qsc", [P, 2, 2, HD])

        ps = ctx.enter_context(nc.psum_tensor("ps", [P, 8, SEQ], FP32))
        psh = [ps[:, i, :].bitcast(FP16) for i in range(8)]

        (A_QKV, A_IN, A_X, G1, G2, MQ, MK, MB, I_QKV, I_IN, I_X, TH1, TH2, NTH1, NTH2, LOGIT, S_H,
         INV_S, EPS_LN, EPS_RMS, IQ, IK, TMP) = range(23)

        def col(i, n=1):
            return sc[:, i:i + n]

        UNITS = 2 * HEADS
        NG = HEADS // GROUP
        PVS = UNITS // GROUP

        def unit(i):
            g, pair, j = i // (2 * GROUP), i // GROUP % 2, i % GROUP
            return g * GROUP + j, 2 * pair

        STATE_BANK = [4, 5, 7]
        Y_BANK = [4, 5, 7, 4]
        QK_BANK = [0, 1, 2, 3, 0, 1, 2, 3]
        V_BANK, QKV_BANK = [2, 2, 3, 3], [0, 1, 2, 3]
        WX_BANK, X_BANK, C_BANK, DT_BANK, RES_BANK = 4, [5, 6, 7, 4], 5, [6, 7, 4, 5], [6, 7, 6, 7]
        n_loads = [0]

        def stand_alone(eng):
            eng.sem_inc(s["waited"], 1)

        def qk_evac(j):
            dst = (qt, kt)[j // 4]
            return dst[:, (j % 4) * 2:(j % 4) * 2 + 2, :], psh[QK_BANK[j]].rearrange("p (a n) -> p a n", a=2)

        def tile_bank(bank, tt):
            return ps[:, bank + tt // 2, (tt % 2) * DIM:(tt % 2 + 1) * DIM]

        def heads_view(flat):
            return flat.rearrange("p (a h d) -> p a h d", a=2 * TT, d=HD)

        names = """ld_w ld_x setup_v setup_p setup_a setup_r setup_t setup_tev setup_ev
                   stats_a mv_a lnv_a rstd_a xn_a xt_a hi_a lo_a stats_b mv_b lnv_b rstd_b xn_b xt_b hi_b lo_b
                   bias_proj bias_f1 bias_f2 bias_out
                   qkv qkv_v qkev vev msq_sq msq_red msq_ln msq_rs qn rot_s ropea roped shifts qhi qlo qktp qkta qktv
                   guard_s guard_m guard_h guard_w guard_t guard_c
                   score prob pv oev otp rden on
                   decay dbu scan htp accd bload0 bload1 bstore
                   ytp yskip y wo woev ontp ocev proj pjev
                   up1 hid1 hhi1 hlo1 down1 fout1 up2 hid2 hhi2 hlo2 down2 fout2
                   xdp xdev ctp cev dtp zc ez lz delta xin mid xcp conv1 conv uu res rescp sres_ du store waited
                   """.split()
        s = {n: sem("s_" + n) for n in names}

        block = ctx.enter_context(nc.Block())

        def iterations(eng, pre, body):
            pre(0)
            body(0, True, False, True)
            with eng.Fori(1, BATCH - 1) as b:
                body(b, True, True, True)
            body(BATCH - 1, True, True, False)
            body(BATCH, False, True, False)

        def ln_set(kind, b):
            if kind == "attn":
                return "a", b if isinstance(b, int) and b < 2 else b * 2 - 2
            if kind == "ffn2":
                return "a", BATCH + b - 1 if isinstance(b, int) and b >= BATCH - 1 else b * 2 + 1
            return "b", b * 2 if kind == "ffn1" else b * 2 + 1

        @block.sync
        def _(sp):
            first = [
                (ldq, t["L0_attn_a_w_qkv"].rearrange("(c p) n -> p c n", p=P)),
                (ldi, t["L0_attn_b_W_in"].rearrange("(c p) n -> p c n", p=P)),
                (ldx, t["L0_attn_b_W_x"].rearrange("(c p) n -> p c n", p=P)),
                (ldw1, t["L0_ffn_W1"].rearrange("(f p) n -> p f n", p=P)),
                (ldw2, t["L0_ffn_W2"].rearrange("(c p) n -> p c n", p=P)),
                (wdt[:, :], t["L0_attn_b_W_dt"]),
                (wproj[:, :, :], t["L0_attn_a_w_proj"].rearrange("(c p) n -> p c n", p=P)),
                (wout[:, :, :], t["L0_attn_b_W_out"].rearrange("(c p) n -> p c n", p=P)),
                (bproj[:, :], t["L0_attn_a_b_proj"].partition_broadcast(P)),
                (bout[:, :], t["L0_attn_b_b_out"].partition_broadcast(P)),
                (b2[:, :], t["L0_ffn_b2"].partition_broadcast(P)),
                (qsc[:, 0, 0, :], t["L0_attn_a_q_scale"].partition_broadcast(P)),
                (qsc[:, 1, 0, :], t["L0_attn_a_k_scale"].partition_broadcast(P)),
                (ropec[:, 0, :, :], cos_t.rearrange("(a p) n -> p a n", p=P)),
                (ropec[:, 1, :, :], cos_t.rearrange("(a p) n -> p a n", p=P)),
                (ropes[:, 0, :, :], sin_t.rearrange("(a p) n -> p a n", p=P)),
                (ropes[:, 1, :, :], sin_t.rearrange("(a p) n -> p a n", p=P)),
                (aneg[:, :, :], t["L0_attn_b_A_log"].rearrange("(c p) n -> p c n", p=P)),
            ]
            for a in range(2):
                name = "L0_attn_a_q_scale" if a == 0 else "L0_attn_a_k_scale"
                for half in range(2):
                    first.append((qsc[:, a, 1, half * HALF:(half + 1) * HALF],
                                  t[name][(1 - half) * HALF:(2 - half) * HALF].partition_broadcast(P)))
            with nc.allow_non_contiguous_dma(reason="small vectors laid over partitions, once"):
                slow = [
                    (b1[:, :], t["L0_ffn_b1"].rearrange("(f p) -> p f", p=P)),
                    (bdt[:, :], t["L0_attn_b_b_dt"].rearrange("(f p) -> p f", p=P)),
                    (bconv[:, :], t["L0_attn_b_b_conv"].rearrange("(f p) -> p f", p=P)),
                    (dskip[:, :], t["L0_attn_b_D"].rearrange("(f p) -> p f", p=P)),
                ] + [(kconv[:, :, j], t["L0_attn_b_K_conv"][j, 0, :].rearrange("(f p) -> p f", p=P))
                     for j in range(CONV)]
                for dst, src in first + slow:
                    sp.dma_start(dst, src).then_inc(s["ld_w"], 16)
            n_loads[0] = len(first + slow)

            def load_b_row(m, n):
                if n >= 2:
                    sp.wait_ge(s["dbu"], m * NS + n - 1)
                    stand_alone(sp)
                sp.dma_start(bbc[:, n % 2, :], bt_scratch[n, :].partition_broadcast(P)).then_inc(s[("bload0", "bload1")[n % 2]], 16)

            def load_x(b):
                sp.dma_start(xa[:, :, :], x_d[b].rearrange("(a p) n -> p a n", p=P)).then_inc(s["ld_x"], 16)

            def body(b, has_a, has_m, has_next):
                if has_m:
                    for n in range(2, NS):
                        load_b_row(b - 1, n)
                if has_next:
                    sp.wait_ge(s["pjev"], (b + 1) * TT)
                    stand_alone(sp)
                    load_x(b + 1)
                if has_a:
                    sp.wait_ge(s["xdev"], b + 1)
                    stand_alone(sp)
                    if has_m:
                        sp.wait_ge(s["dbu"], b * NS)
                    sp.dma_start(bt_scratch[:, :], xdbl[RANK:RANK + NS, :]).then_inc(s["bstore"], 16)
                    sp.wait_ge(s["bstore"], (b + 1) * 16)
                    stand_alone(sp)
                    for n in range(2):
                        load_b_row(b, n)
                if has_m:
                    sp.wait_ge(s["fout2"], b * TT)
                    stand_alone(sp)
                    sp.dma_start(y_d[b - 1].rearrange("(a p) n -> p a n", p=P), yo[:, :, :]).then_inc(s["store"], 16)

            iterations(sp, load_x, body)
            sp.wait_ge(s["store"], 16 * (BATCH + 1))

        @block.gpsimd
        def _(pool):
            nc.gpsimd.memset(identf[:, :], 0.0).then_inc(s["setup_p"], 1)
            nc.gpsimd.memset(identh[:, :], 0.0).then_inc(s["setup_p"], 1)
            pool.wait_ge(s["setup_p"], 2)
            for m in (identf, identh):
                nc.gpsimd.affine_select(out=m[:, :], in_=m[:, :], compare_op=ALU.not_equal, fill=1.0,
                                        base=0, pattern=[[-1, P]], channel_multiplier=1).then_inc(s["setup_p"], 1)
            nc.gpsimd.memset(vaug[:, :, :, HD:2 * HD], 1.0).then_inc(s["setup_p"], 1)
            nc.gpsimd.memset(ones8[:, :], 1.0).then_inc(s["setup_p"], 1)
            nc.gpsimd.memset(decay[:, :, :, 0:1], 0.0).then_inc(s["setup_p"], 1)
            nc.gpsimd.memset(yo[:, 0, 0:1], 0.0).then_inc(s["store"], 16)

            def add_bias(dst, bias, kind, b, done):
                st, i = ln_set(kind, b)
                pool.wait_ge(s["xn_" + st], i + 1)
                nc.gpsimd.tensor_tensor(dst[:, :, :], dst[:, :, :],
                                        bias[:, :].unsqueeze(1).to_broadcast([P, TT, DIM]),
                                        ALU.add).then_inc(s[done], 1)

            def q_k_rotated(b):
                pool.wait_ge(s["msq_rs"], b + 1)
                nc.gpsimd.tensor_tensor(
                    qn.rearrange("p (a d) -> p a d", d=HD),
                    qk.rearrange("p a (h d) -> p (a h) d", d=HD),
                    rms[:, :].unsqueeze(2).to_broadcast([P, 2 * TT * HEADS, HD]), ALU.mult).then_inc(s["qn"], 1)
                pool.wait_ge(s["qn"], b + 1)
                s3 = ropes[:, :, :, :].rearrange("p a b d -> p (a b) d")
                for half in range(2):
                    to, frm = half * HALF, (1 - half) * HALF
                    nc.gpsimd.tensor_tensor(
                        heads_view(rot)[:, :, :, to:to + HALF], heads_view(qn)[:, :, :, frm:frm + HALF],
                        s3[:, :, to:to + HALF].unsqueeze(2).to_broadcast([P, 2 * TT, HEADS, HALF]),
                        ALU.mult).then_inc(s["rot_s"], 1)
                pool.wait_ge(s["rot_s"], 2 * (b + 1))
                pool.wait_ge(s["ropea"], b + 1)
                nc.gpsimd.tensor_tensor(rot, sq, rot, ALU.add).then_inc(s["roped"], 1)
                pool.wait_ge(s["roped"], b + 1)
                stand_alone(pool)
                for a in range(2):
                    nc.gpsimd.memset(qka[:, a, :, SHIFT:ROWS], float(a)).then_inc(s["shifts"], 1)

            def pre(b):
                add_bias(xa, bproj, "attn", b, "bias_proj")
                q_k_rotated(b)

            def body(b, has_a, has_m, has_next):
                if has_m:
                    pool.wait_ge(s["du"], b * DT)
                    pool.wait_ge(s["down2"], b)
                    for n in range(NS):
                        pool.wait_ge(s[("bload0", "bload1")[n % 2]], ((b - 1) * (NS // 2) + n // 2 + 1) * 16)
                        if n >= HSLOTS:
                            pool.wait_ge(s["htp"], ((b - 1) * NS + n - HSLOTS + 1) * TT)
                        nc.gpsimd.tensor_tensor(
                            hst[:, n % HSLOTS, :, :], du[:, :, :],
                            bbc[:, n % 2, :].unsqueeze(1).to_broadcast([P, DT, SEQ]), ALU.mult).then_inc(s["dbu"], 1)
                        if n == 3:
                            pool.wait_ge(s["fout1"], b * TT)
                            pool.wait_ge(s["store"], 16 * b)
                            nc.gpsimd.tensor_tensor(yo[:, :, :], xb[:, :, :],
                                                    bout[:, :].unsqueeze(1).to_broadcast([P, TT, DIM]),
                                                    ALU.add).then_inc(s["bias_out"], 1)
                    pool.wait_ge(s["sres_"], b)
                    for d in range(DT):
                        pool.wait_ge(s["yskip"], (b - 1) * DT + d + 1)
                        nc.gpsimd.tensor_tensor(ybuf[:, d, :], ybuf[:, d, :], sres[:, d, :], ALU.mult).then_inc(s["y"], 1)
                if has_a:
                    add_bias(xb, b2, "ffn1", b, "bias_f1")
                if has_next:
                    add_bias(xa, bproj, "attn", b + 1, "bias_proj")
                if has_m:
                    add_bias(yo, b2, "ffn2", b, "bias_f2")
                if has_next:
                    q_k_rotated(b + 1)

            iterations(pool, pre, body)

        @block.scalar
        def _(act):
            nc.scalar.preload_act_table_set(EXP_LN)
            act.wait_ge(s["ld_w"], 16 * n_loads[0])
            nc.scalar.activation(aneg[:, :, :], aneg[:, :, :], ACT.Exp).then_inc(s["setup_a"], 1)
            act.wait_ge(s["setup_v"], 3)

            def ln_scale(kind, b):
                st, i = ln_set(kind, b)
                w = LN[st][0]
                act.wait_ge(s["mv_" + st], i + 1)
                nc.scalar.activation(lnv[:, w, :], mv[:, w, :, 1], ACT.Ln, bias=col(EPS_LN)).then_inc(s["lnv_" + st], 1)
                act.wait_ge(s["lnv_" + st], i + 1)
                nc.scalar.activation(rstd[:, w, :], lnv[:, w, :], ACT.Exp, scale=-0.5).then_inc(s["rstd_" + st], 1)

            def ln_high(kind, b):
                st, i = ln_set(kind, b)
                _, _, xt, (bank, _) = LN[st]
                act.wait_ge(s["xt_" + st], i + 1)
                nc.scalar.activation(xt[:, 0, :, :], ps[:, bank:bank + 2, :], ACT.Copy).then_inc(s["hi_" + st], 1)

            def hidden_chunk(which, i, f):
                bank = (None, 6, 2)[which] + f % 2
                act.wait_ge(s[f"up{which}"], i * FC + f + 1)
                if f >= 4:
                    act.wait_ge(s[f"hlo{which}"], i * FC + f - 3)
                nc.scalar.activation(hid[:, f % 4, :], ps[:, bank, :], ACT.Relu,
                                     bias=b1[:, f:f + 1], scale=col(S_H)).then_inc(s[f"hid{which}"], 1)
                nc.scalar.activation(h_hi[:, f, :], ps[:, bank, :], ACT.Relu,
                                     bias=b1[:, f:f + 1], scale=col(S_H)).then_inc(s[f"hhi{which}"], 1)

            def qkv_out(b, tt):
                q4 = qk.rearrange("p (a b) n -> p a b n", a=2)
                s4 = sq.rearrange("p (a b n) -> p a b n", a=2, b=TT)
                act.wait_ge(s["qkv"], b * TT + tt + 1)
                pq = ps[:, QKV_BANK[tt], :].rearrange("p (a n) -> p a n", a=2)
                nc.scalar.activation(q4[:, :, tt, :], pq, ACT.Copy, scale=col(A_QKV)).then_inc(s["qkev"], 1)
                nc.scalar.activation(s4[:, :, tt, :], pq, ACT.Square, scale=col(A_QKV)).then_inc(s["msq_sq"], 1)

            def rms_scale(b):
                act.wait_ge(s["msq_red"], b + 1)
                nc.scalar.activation(msq[:, :], msq[:, :], ACT.Ln, bias=col(EPS_RMS), scale=1.0 / HD).then_inc(s["msq_ln"], 1)
                act.wait_ge(s["msq_ln"], b + 1)
                nc.scalar.activation(rms[:, :], msq[:, :], ACT.Exp, scale=-0.5).then_inc(s["msq_rs"], 1)

            def qk_high(b):
                act.wait_ge(s["roped"], b + 1)
                for a in range(2):
                    step = 2 - a
                    src = rot[:, a * TT * DIM:(a + 1) * TT * DIM].rearrange("p (h d) -> p h d", d=HD)
                    for c in range(2):
                        o = c * step * HD
                        nc.scalar.activation(qka[:, a, :, o:o + HD], src, ACT.Copy).then_inc(s["qhi"], 1)

            def qk_even(b):
                for j in range(0, 8, 2):
                    act.wait_ge(s["qktp"], b * 8 + j + 1)
                    nc.scalar.activation(*qk_evac(j), ACT.Copy).then_inc(s["qkta"], 1)

            def pre(b):
                ln_scale("attn", b)
                ln_high("attn", b)
                for tt in range(TT):
                    qkv_out(b, tt)
                rms_scale(b)
                qk_high(b)
                qk_even(b)

            def x_out(b, d):
                act.wait_ge(s["xin"], b * DT + d + 1)
                nc.scalar.activation(u[:, d, :], ps[:, X_BANK[d], :], ACT.Copy, scale=kmid[:, d:d + 1]).then_inc(s["mid"], 1)
                nc.scalar.activation(xs[:, d, :], ps[:, X_BANK[d], :], ACT.Copy, scale=col(A_IN)).then_inc(s["xcp"], 1)

            def softplus_exp(b, d):
                act.wait_ge(s["zc"], b * DT + d + 1)
                nc.scalar.activation(zs[:, d, :], zs[:, d, :], ACT.Exp).then_inc(s["ez"], 1)

            def softplus_ln(b):
                for d in range(DT):
                    act.wait_ge(s["ez"], b * DT + d + 1)
                    nc.scalar.activation(zs[:, d, :], zs[:, d, :], ACT.Ln, bias=1.0).then_inc(s["lz"], 1)

            def res_out(b, d):
                act.wait_ge(s["res"], b * DT + d + 1)
                nc.scalar.activation(sres[:, d, :], ps[:, RES_BANK[d], :], ACT.Copy, scale=col(A_IN)).then_inc(s["rescp"], 1)

            def body(b, has_a, has_m, has_next):
                def decays(m, n):
                    if n == 0:
                        act.wait_ge(s["delta"], (m + 1) * DT)
                    if n >= 2:
                        act.wait_ge(s["scan"], m * NS + n - 1)
                    for d in range(DT):
                        ins = nc.scalar.activation(decay[:, n % 2, d, 1:SEQ], delta[:, d, 1:SEQ], ACT.Exp,
                                                   scale=aneg[:, d, n:n + 1])
                    ins.then_inc(s["decay"], 1)

                def numerators(i):
                    act.wait_ge(s["score"], b * UNITS + i + 1)
                    if i >= PSLOTS:
                        act.wait_ge(s["pv"], b * PVS + (i - PSLOTS) // GROUP + 1)
                    bank = 2 * (i % 2)
                    nc.scalar.activation(prob[:, i % PSLOTS, :, :], ps[:, bank:bank + 2, :], ACT.Exp,
                                         scale=col(LOGIT)).then_inc(s["prob"], 1)

                for n in range(1, NS + LAG):
                    if has_m and n + 1 < NS:
                        decays(b - 1, n + 1)
                    if has_m and n == 1:
                        act.wait_ge(s["rescp"], b * DT)
                        nc.scalar.activation(sres[:, :, :], sres[:, :, :], ACT.Silu).then_inc(s["sres_"], 1)
                        nc.scalar.preload_act_table_set(EXP_LN)
                    if has_a and n >= LAG:
                        numerators(2 * (n - LAG))
                        numerators(2 * (n - LAG) + 1)
                if has_a:
                    act.wait_ge(s["ontp"], b + 1)
                    nc.scalar.activation(oc, ps[:, 4:6, :], ACT.Copy).then_inc(s["ocev"], 1)
                    ln_scale("ffn1", b)
                    ln_high("ffn1", b)
                    for f in range(FC):
                        if has_next and f == 2:
                            ln_scale("attn", b + 1)
                        if has_next and f == 4:
                            ln_high("attn", b + 1)
                        if has_m and f == 6:
                            ln_scale("ffn2", b)
                        if has_next and f == 7:
                            qkv_out(b + 1, 0)
                        hidden_chunk(1, b, f)
                    if has_next:
                        for tt in range(1, TT):
                            qkv_out(b + 1, tt)
                elif has_m:
                    ln_scale("ffn2", b)
                if has_m:
                    ln_high("ffn2", b)
                if has_a:
                    ln_scale("scan", b)
                for f in range(FC):
                    if has_a and f == 2:
                        ln_high("scan", b)
                    if has_next and f == 3:
                        rms_scale(b + 1)
                    if has_a and f == 3:
                        act.wait_ge(s["xdp"], b + 1)
                        if has_m:
                            act.wait_ge(s["bstore"], 16 * b)
                        nc.scalar.activation(xdbl[:, :], ps[0:XD, WX_BANK, :], ACT.Copy, scale=sc[0:XD, A_X:A_X + 1]).then_inc(s["xdev"], 1)
                    if has_a and f in (3, 4):
                        x_out(b, 2 * (f - 3))
                        x_out(b, 2 * (f - 3) + 1)
                    if has_a and f in (6, 7):
                        softplus_exp(b, 2 * (f - 6))
                        softplus_exp(b, 2 * (f - 6) + 1)
                    if has_a and f == 7:
                        softplus_ln(b)
                    if has_next and f == QK_HIGH_AT:
                        qk_high(b + 1)
                    if has_m:
                        hidden_chunk(2, b - 1, f)
                if has_a:
                    for d in range(DT):
                        act.wait_ge(s["conv"], b * DT + d + 1)
                        nc.scalar.activation(u[:, d, :], u[:, d, :], ACT.Silu, bias=bconv[:, d:d + 1]).then_inc(s["uu"], 1)
                    res_out(b, 0)
                    res_out(b, 1)
                    nc.scalar.preload_act_table_set(EXP_LN)
                    decays(b, 0)
                    res_out(b, 2)
                    res_out(b, 3)
                    decays(b, 1)
                if has_next:
                    qk_even(b + 1)

            iterations(act, pre, body)

        @block.vector
        def _(dve):
            v = nc.vector
            dve.wait_ge(s["ld_w"], 16 * n_loads[0])
            dve.wait_ge(s["setup_p"], 7)
            k = [0]

            def link(ins):
                k[0] += 1
                ins.then_inc(s["setup_ev"], 1)
                dve.wait_ge(s["setup_ev"], k[0])

            for i, src, op in ((A_QKV, ldq, ALU.max), (A_IN, ldi, ALU.max), (A_X, ldx, ALU.max),
                               (G1, ldw1, ALU.add), (G2, ldw2, ALU.add)):
                v.tensor_reduce(col(i), src, AX.XY, op, apply_absolute_value=True)
            v.tensor_reduce(col(MQ), qsc[:, 0, 0, :], AX.X, ALU.max, apply_absolute_value=True)
            v.tensor_reduce(col(MK), qsc[:, 1, 0, :], AX.X, ALU.max, apply_absolute_value=True)
            v.memset(col(EPS_LN), LN_EPS)
            v.memset(col(EPS_RMS), RMS_EPS)
            v.tensor_reduce(col(MB), b1[:, :], AX.X, ALU.max, apply_absolute_value=True).then_inc(s["setup_v"], 1)
            dve.wait_ge(s["setup_p"], 4)
            dve.wait_ge(s["setup_r"], 1)
            link(v.tensor_reduce(red[:, 0:1], ps[0:8, 0, 0:P], AX.X, ALU.max))
            link(v.tensor_reduce(red[:, 1:2], ps[0:8, 0, 0:P], AX.X, ALU.add))
            link(v.tensor_scalar(reddiag[:, 0:8], identf[0:8, 0:8], red[:, 0:1], None, ALU.mult))
            v.tensor_scalar(reddiag[:, 8:16], identf[0:8, 0:8], red[:, 1:2], None, ALU.mult).then_inc(s["setup_v"], 1)
            dve.wait_ge(s["setup_r"], 2)
            link(v.tensor_copy(col(0, 3), ps[:, 1, 0:3]))
            link(v.tensor_copy(col(G1, 2), ps[:, 1, 8 + G1:8 + G1 + 2]))
            link(v.tensor_copy(col(MB), ps[:, 1, MB:MB + 1]))
            link(v.tensor_scalar(col(A_QKV, 3), col(A_QKV, 3), 1e-30, None, ALU.max))
            link(v.tensor_scalar(col(MQ, 2), col(MQ, 2), 1e-30, None, ALU.max))
            link(v.reciprocal(col(I_QKV, 3), col(A_QKV, 3)))
            link(v.reciprocal(col(IQ, 2), col(MQ, 2)))
            link(v.tensor_tensor(col(TMP), col(MQ), col(MK), ALU.mult))
            link(v.tensor_scalar(col(LOGIT), col(TMP), float(HD) ** -0.5, None, ALU.mult))
            link(v.tensor_scalar(big_logits[:, :], col(LOGIT), MAX_LOGIT_UNSHIFTED / HD, None, ALU.is_gt))
            link(v.tensor_scalar(col(TH1, 2), col(G1, 2), 1.0 / (FF * DIM), Q_EPS, ALU.mult, ALU.add))
            link(v.tensor_scalar(col(NTH1, 2), col(TH1, 2), -0.5, None, ALU.mult))
            link(v.tensor_scalar(col(TH1, 2), col(TH1, 2), 0.5, None, ALU.mult))
            link(v.tensor_scalar(col(INV_S), col(MB), 1.0 / LN_BOUND, 1.0, ALU.mult, ALU.add))
            link(v.reciprocal(col(S_H), col(INV_S)))
            link(v.tensor_scalar(b1[:, :], b1[:, :], col(S_H), None, ALU.mult))
            for i, src, hi_, lo_ in ((I_QKV, ldq, wqkv_hi, wqkv_lo), (I_IN, ldi, win_hi, win_lo), (I_X, ldx, wx_hi, wx_lo)):
                link(v.tensor_scalar(src, src, col(i), None, ALU.mult))
                link(v.tensor_copy(hi_[:, :, :], src))
                link(v.tensor_tensor(lo_[:, :, :], src, hi_[:, :, :], ALU.subtract))
            for thr, nthr, src, dst in ((TH1, NTH1, ldw1, tern1), (TH2, NTH2, ldw2, tern2)):
                tmp = stmp.rearrange("p (f n) -> p f n", f=src.shape[1])
                link(v.tensor_scalar(tmp, src, col(nthr), None, ALU.is_lt))
                link(v.scalar_tensor_tensor(dst, src, col(thr), tmp, ALU.is_gt, ALU.subtract))
            for a in range(2):
                for tab, w in ((ropec, 0), (ropes, 1)):
                    link(v.tensor_scalar(qsc[:, a, w, :], qsc[:, a, w, :], col(IQ + a), None, ALU.mult))
                    link(v.tensor_tensor(tab[:, a, :, :], tab[:, a, :, :],
                                         qsc[:, a, w, :].unsqueeze(1).to_broadcast([P, TT, HD]), ALU.mult))
            link(v.tensor_scalar(kmid[:, :], kconv[:, :, PAD], col(A_IN), None, ALU.mult))
            dve.wait_ge(s["setup_a"], 1)
            v.tensor_scalar(aneg[:, :, :], aneg[:, :, :], -1.0, None, ALU.mult).then_inc(s["setup_v"], 1)
            for f in range(8):
                dve.wait_ge(s["setup_t"], f + 1)
                if f < 4:
                    dst = w1t[:, f // 2, (f % 2) * 512:(f % 2) * 512 + 512]
                    v.tensor_copy(dst, psh[f][:, 0:512]).then_inc(s["setup_tev"], 1)
                else:
                    g = f - 4
                    v.tensor_copy(w2t[:, 2 * g:2 * g + 2, :],
                                  psh[f][:, 0:512].rearrange("p (a n) -> p a n", a=2)).then_inc(s["setup_tev"], 1)

            need_max = dve.value_load(big_logits[0:1, 0:1])

            def guard(b):
                n = HEADS * TT
                for j in range(n):
                    h, tt = j // TT, j % TT
                    dve.wait_ge(s["guard_s"], b * n + j + 1)
                    v.reduce_max(rowmax[:, tt * HEADS + h:tt * HEADS + h + 1], ps[:, j % 4, :], AX.X).then_inc(s["guard_m"], 1)
                dve.wait_ge(s["guard_m"], (b + 1) * n)
                v.tensor_scalar(qka[:, 0, :, SHIFT], rowmax[:, :], -1.0, None, ALU.mult).then_inc(s["guard_h"], 1)
                dve.wait_ge(s["guard_h"], b + 1)
                v.scalar_tensor_tensor(qka[:, 0, :, SHIFT + 1], rowmax[:, :], -1.0, qka[:, 0, :, SHIFT],
                                       ALU.mult, ALU.subtract).then_inc(s["guard_w"], 1)
                for j in range(4):
                    dve.wait_ge(s["guard_t"], b * 4 + j + 1)
                    v.tensor_copy(*qk_evac(j)).then_inc(s["guard_c"], 1)

            def ln_stats(kind, b, src):
                st, i = ln_set(kind, b)
                w = LN[st][0]
                for tt in range(TT):
                    ins = v.bn_stats(bnst[:, w, tt, :], src[:, tt, :])
                ins.then_inc(s["stats_" + st], 1)
                dve.wait_ge(s["stats_" + st], i + 1)
                stand_alone(dve)
                for tt in range(TT):
                    ins = v.bn_aggr(mv[:, w, tt, :], bnst[:, w, tt, :])
                ins.then_inc(s["mv_" + st], 1)

            def ln_norm(kind, b, src):
                st, i = ln_set(kind, b)
                w, rows, _, _ = LN[st]
                dve.wait_ge(s["rstd_" + st], i + 1)
                for tt in range(TT):
                    ins = v.tensor_scalar(rows[:, tt, :], src[:, tt, :], mv[:, w, tt, 0:1], rstd[:, w, tt:tt + 1],
                                          ALU.subtract, ALU.mult)
                ins.then_inc(s["xn_" + st], 1)

            def ln_low(kind, b):
                st, i = ln_set(kind, b)
                _, _, xt, (bank, _) = LN[st]
                dve.wait_ge(s["hi_" + st], i + 1)
                v.tensor_tensor(xt[:, 1, :, :], ps[:, bank:bank + 2, :], xt[:, 0, :, :], ALU.subtract).then_inc(s["lo_" + st], 1)

            def hidden_low(which, i, f):
                dve.wait_ge(s[f"hhi{which}"], i * FC + f + 1)
                v.tensor_tensor(h_lo[:, f, :], hid[:, f % 4, :], h_hi[:, f, :], ALU.subtract).then_inc(s[f"hlo{which}"], 1)

            def ffn_out(which, i, rows, bias):
                dve.wait_ge(s[f"down{which}"], i + which)
                dve.wait_ge(s[bias], i + 1)
                for tt in range(TT):
                    v.scalar_tensor_tensor(rows[:, tt, :], tile_bank((None, 4, 0)[which], tt), col(INV_S), rows[:, tt, :],
                                           ALU.mult, ALU.add).then_inc(s[f"fout{which}"], 1)

            def scan_step(m, n):
                dve.wait_ge(s["decay"], m * NS + n + 1)
                dve.wait_ge(s["dbu"], m * NS + n + 1)
                flat = hst[:, n % HSLOTS, :, :].rearrange("p d t -> p (d t)")
                v.tensor_tensor_scan(flat, decay[:, n % 2, :, :].rearrange("p d t -> p (d t)"), flat, 0.0,
                                     ALU.mult, ALU.add).then_inc(s["scan"], 1)

            def acc_step(m, n):
                for tt in range(TT):
                    dve.wait_ge(s["htp"], (m * NS + n) * TT + tt + 1)
                    src = ps[:, STATE_BANK[(n * TT + tt) % 3], :]
                    if n == 0:
                        ins = v.tensor_scalar(acc[:, tt, :], src, ctok[:, tt, n:n + 1], None, ALU.mult)
                    else:
                        ins = v.scalar_tensor_tensor(acc[:, tt, :], src, ctok[:, tt, n:n + 1], acc[:, tt, :],
                                                     ALU.mult, ALU.add)
                    ins.then_inc(s["accd"], 1)

            def group_out(b, g):
                dve.wait_ge(s["pv"], b * PVS + 2 * g + 2)
                if g >= 1:
                    dve.wait_ge(s["otp"], b * NG + g)
                v.tensor_copy(ot, ps[:, 6, :]).then_inc(s["oev"], 1)

            def group_norm(b, g):
                dve.wait_ge(s["otp"], b * NG + g + 1)
                o4 = ps[:, 6, :].rearrange("p (t j r) -> p t j r", t=TT, j=GROUP)
                v.reciprocal(rden[:, :, :], o4[:, :, :, HD]).then_inc(s["rden"], 1)
                dve.wait_ge(s["rden"], b * NG + g + 1)
                v.tensor_tensor(on[:, :, g * GROUP * HD:(g + 1) * GROUP * HD].rearrange("p t (j d) -> p t j d", j=GROUP),
                                o4[:, :, :, 0:HD], rden[:, :, :].unsqueeze(3).to_broadcast([P, TT, GROUP, HD]),
                                ALU.mult).then_inc(s["on"], 1)

            def values_out(b):
                for tt in range(TT):
                    dve.wait_ge(s["qkv_v"], b * TT + tt // 2 * 2 + 2)
                    v.tensor_scalar(vaug[:, tt, :, 0:HD], tile_bank(V_BANK[0], tt).rearrange("p (h d) -> p h d", d=HD),
                                    col(A_QKV), None, ALU.mult).then_inc(s["vev"], 1)

            def mean_squares(b):
                dve.wait_ge(s["msq_sq"], (b + 1) * TT)
                v.tensor_reduce(msq[:, :], sq.rearrange("p (a d) -> p a d", d=HD), AX.X, ALU.add).then_inc(s["msq_red"], 1)

            def rope_cos(b):
                dve.wait_ge(s["qn"], b + 1)
                v.tensor_tensor(heads_view(sq), heads_view(qn),
                                ropec[:, :, :, :].rearrange("p a b d -> p (a b) d").unsqueeze(2)
                                .to_broadcast([P, 2 * TT, HEADS, HD]), ALU.mult).then_inc(s["ropea"], 1)

            def qk_low(b):
                dve.wait_ge(s["qhi"], 4 * (b + 1))
                for a in range(2):
                    o = (1 + a) * HD
                    src = rot[:, a * TT * DIM:(a + 1) * TT * DIM].rearrange("p (h d) -> p h d", d=HD)
                    v.tensor_tensor(qka[:, a, :, o:o + HD], src, qka[:, a, :, 0:HD], ALU.subtract).then_inc(s["qlo"], 1)

            def qk_odd(b):
                for j in range(1, 8, 2):
                    dve.wait_ge(s["qktp"], b * 8 + j + 1)
                    v.tensor_copy(*qk_evac(j)).then_inc(s["qktv"], 1)

            def qk_guard(b):
                with dve.If(need_max == 1):
                    guard(b)
                with dve.Else():
                    dve.sem_inc(s["waited"], 1)

            def pre(b):
                dve.wait_ge(s["ld_x"], 16 * (b + 1))
                ln_stats("attn", b, xa)
                ln_norm("attn", b, xa)
                ln_low("attn", b)
                values_out(b)
                mean_squares(b)
                rope_cos(b)
                qk_low(b)
                qk_odd(b)
                qk_guard(b)

            def conv_tile(b, d):
                dve.wait_ge(s["mid"], b * DT + d + 1)
                dve.wait_ge(s["xcp"], b * DT + d + 1)
                others = [j for j in range(CONV) if j != PAD]
                for i, j in enumerate(others):
                    if i > 0:
                        dve.wait_ge(s["conv1"], (b * DT + d) * (len(others) - 1) + i)
                    o = j - PAD
                    to, frm = slice(max(0, -o), SEQ - max(0, o)), slice(max(0, o), SEQ + min(0, o))
                    v.scalar_tensor_tensor(u[:, d, to], xs[:, d, frm], kconv[:, d, j:j + 1], u[:, d, to], ALU.mult,
                                           ALU.add).then_inc(s["conv1"] if i + 1 < len(others) else s["conv"], 1)

            def body(b, has_a, has_m, has_next):
                m = b - 1
                for n in range(NS + 1 + LAG):
                    k = n - LAG
                    if has_m and 0 < n < NS:
                        scan_step(m, n)
                    if has_a and k > GROUP and k % GROUP == 1:
                        group_out(b, k // GROUP - 1)
                    if has_m and 0 < n <= NS:
                        acc_step(m, n - 1)
                    if has_a and k > GROUP and k % GROUP == 2:
                        group_norm(b, k // GROUP - 1)
                    if has_m and n == NS + 1:
                        for d in range(DT):
                            dve.wait_ge(s["ytp"], m * DT + d + 1)
                            v.scalar_tensor_tensor(ybuf[:, d, :], u[:, d, :], dskip[:, d:d + 1], ps[:, Y_BANK[d], :],
                                                   ALU.mult, ALU.add).then_inc(s["yskip"], 1)
                if has_a:
                    group_out(b, NG - 1)
                if has_a:
                    group_norm(b, NG - 1)
                    dve.wait_ge(s["bias_proj"], b + 1)
                    if has_m:
                        dve.wait_ge(s["bias_out"], b)
                    for tt in range(TT):
                        dve.wait_ge(s["proj"], b * TT + tt // 2 * 2 + 2)
                        v.tensor_tensor(xb[:, tt, :], tile_bank(6, tt), xa[:, tt, :], ALU.add).then_inc(s["pjev"], 1)
                    dve.wait_ge(s["pjev"], (b + 1) * TT)
                    ln_stats("ffn1", b, xb)
                    ln_norm("ffn1", b, xb)
                if has_m:
                    dve.wait_ge(s["bias_out"], b)
                    for tt in range(TT):
                        dve.wait_ge(s["wo"], m * TT + tt // 2 * 2 + 2)
                        v.tensor_tensor(yo[:, tt, :], tile_bank(2, tt), yo[:, tt, :], ALU.add).then_inc(s["woev"], 1)
                    dve.wait_ge(s["woev"], b * TT)
                if has_a:
                    ln_low("ffn1", b)
                    for f in range(FC):
                        if has_next and f == 1:
                            dve.wait_ge(s["ld_x"], 16 * (b + 2))
                            ln_stats("attn", b + 1, xa)
                        if has_next and f == 3:
                            ln_norm("attn", b + 1, xa)
                        if has_next and f == 4:
                            ln_low("attn", b + 1)
                        if has_m and f == 5:
                            ln_stats("ffn2", b, yo)
                        if has_next and f == 6:
                            values_out(b + 1)
                        if has_m and f == 7:
                            ln_norm("ffn2", b, yo)
                        hidden_low(1, b, f)
                    ffn_out(1, b, xb, "bias_f1")
                    dve.wait_ge(s["fout1"], (b + 1) * TT)
                    ln_stats("scan", b, xb)
                else:
                    ln_stats("ffn2", b, yo)
                    ln_norm("ffn2", b, yo)
                if has_m:
                    ln_low("ffn2", b)
                if has_a:
                    ln_norm("scan", b, xb)
                for f in range(FC):
                    if has_a and f == 2:
                        ln_low("scan", b)
                    if has_next and f == 2:
                        mean_squares(b + 1)
                    if has_next and f == ROPE_AT:
                        rope_cos(b + 1)
                    if has_a and f in (3, 4):
                        conv_tile(b, f - 3)
                    if has_a and f == 5:
                        dve.wait_ge(s["ctp"], b + 1)
                        v.tensor_copy(ctok[:, :, :], ps[:, C_BANK, :].rearrange("p (t r) -> p t r", t=TT)[:, :, RANK + NS:XD]).then_inc(s["cev"], 1)
                    if has_a and f in (5, 6):
                        for d in range(2 * (f - 5), 2 * (f - 5) + 2):
                            dve.wait_ge(s["dtp"], b * DT + d + 1)
                            v.tensor_scalar(zs[:, d, :], ps[:, DT_BANK[d], :], bdt[:, d:d + 1], 30.0, ALU.add, ALU.min).then_inc(s["zc"], 1)
                    if has_a and f in (5, 6):
                        conv_tile(b, f - 3)
                    if has_a and f == 7:
                        for d in range(DT):
                            dve.wait_ge(s["lz"], b * DT + d + 1)
                            v.scalar_tensor_tensor(delta[:, d, :], ps[:, DT_BANK[d], :], bdt[:, d:d + 1], zs[:, d, :],
                                                   ALU.add, ALU.max).then_inc(s["delta"], 1)
                    if has_m:
                        hidden_low(2, m, f)
                if has_a:
                    for d in range(DT):
                        dve.wait_ge(s["delta"], b * DT + d + 1)
                        dve.wait_ge(s["uu"], b * DT + d + 1)
                        v.tensor_tensor(du[:, d, :], delta[:, d, :], u[:, d, :], ALU.mult).then_inc(s["du"], 1)
                if has_next:
                    qk_low(b + 1)
                if has_m:
                    ffn_out(2, m, yo, "bias_f2")
                if has_a:
                    scan_step(b, 0)
                if has_next:
                    qk_odd(b + 1)
                    qk_guard(b + 1)

            iterations(dve, pre, body)

        @block.tensor
        def _(pe):
            mm, tp = nc.tensor.matmul, nc.tensor.transpose
            pe.wait_ge(s["setup_p"], 7)
            pe.wait_ge(s["setup_v"], 1)
            tp(ps[0:8, 0, 0:P], sc[:, 0:8], identf[:, :]).then_inc(s["setup_r"], 1)
            pe.wait_ge(s["setup_v"], 2)
            mm(ps[:, 1, 0:16], ones8[:, :], reddiag[:, :], start=True, stop=True).then_inc(s["setup_r"], 1)
            pe.wait_ge(s["setup_v"], 3)
            for f in range(4):
                c, base = f // 2, (f % 2) * 4
                for i in range(4):
                    ins = tp(psh[f][:, i * P:(i + 1) * P], tern1[:, base + i, c * P:(c + 1) * P], identh[:, :])
                ins.then_inc(s["setup_t"], 1)
            for g in range(4):
                for i in range(4):
                    ins = tp(psh[4 + g][:, i * P:(i + 1) * P],
                             tern2[:, i % 2, (2 * g + i // 2) * P:(2 * g + i // 2 + 1) * P], identh[:, :])
                ins.then_inc(s["setup_t"], 1)
            pe.wait_ge(s["setup_tev"], 8)

            need_max = pe.value_load(big_logits[0:1, 0:1])

            def q_or_k_transposes(j):
                bank = QK_BANK[j]
                for e in range(2):
                    hp = (j % 4) * 2 + e
                    for tt in range(TT):
                        o = e * SEQ + tt * P
                        src = qka[:, j // 4, tt * HEADS + 2 * hp:tt * HEADS + 2 * hp + 2, :].rearrange("p h r -> p (h r)")
                        ins = tp(psh[bank][:, o:o + P], src, identh[:, :])
                return ins

            def guard(b):
                n = HEADS * TT
                for j in range(n):
                    h, tt = j // TT, j % TT
                    r, hp = (h % 2) * ROWS, h // 2
                    if j >= 4:
                        pe.wait_ge(s["guard_m"], b * n + j - 3)
                    mm(ps[:, j % 4, :], qt[r:r + ROWS, hp, tt * P:(tt + 1) * P], kt[r:r + ROWS, hp, :],
                       start=True, stop=True).then_inc(s["guard_s"], 1)
                pe.wait_ge(s["guard_w"], b + 1)
                for j in range(4):
                    q_or_k_transposes(j).then_inc(s["guard_t"], 1)
                pe.wait_ge(s["guard_c"], 4 * (b + 1))

            def ln_transposes(kind, b):
                st, i = ln_set(kind, b)
                _, rows, _, banks = LN[st]
                pe.wait_ge(s["xn_" + st], i + 1)
                for c in range(KC):
                    for tt in range(TT):
                        ins = tp(ps[:, banks[c], tt * P:(tt + 1) * P], rows[:, tt, c * P:(c + 1) * P], identf[:, :])
                ins.then_inc(s["xt_" + st], 1)

            def ln_done(kind, b):
                st, i = ln_set(kind, b)
                pe.wait_ge(s["lo_" + st], i + 1)

            def ffn(which, i, kind, b, between):
                xt = LN[ln_set(kind, b)[0]][2]
                up_bank, out_bank = (None, (6, 4), (2, 0))[which]
                st, n = ln_set(kind, b)
                pe.wait_ge(s["hi_" + st], n + 1)

                def up(f):
                    if f >= 2:
                        pe.wait_ge(s[f"hhi{which}"], i * FC + f - 1)
                    for part in range(2):
                        if f == 0 and part == 1:
                            ln_done(kind, b)
                        for c in range(KC):
                            ins = mm(ps[:, up_bank + f % 2, :], w1t[:, c, f * P:(f + 1) * P], xt[:, part, c, :],
                                     start=(c + part == 0), stop=(c + part == KC))
                    ins.then_inc(s[f"up{which}"], 1)

                def down(f):
                    pe.wait_ge(s[f"hlo{which}"], i * FC + f + 1)
                    for tt in range(TT):
                        for part, h in enumerate((h_hi, h_lo)):
                            ins = mm(tile_bank(out_bank, tt), h[:, f, tt * P:(tt + 1) * P], w2t[:, f, :],
                                     start=(f == 0 and part == 0 and tt % 2 == 0),
                                     stop=(f == FC - 1 and part == 1 and tt % 2 == 1), skip_group_check=True)
                    return ins

                for f in range(FC + 2):
                    for step in between.get(f, []):
                        step()
                    if f < FC:
                        up(f)
                    if f >= 2:
                        ins = down(f - 2)
                ins.then_inc(s[f"down{which}"], 1)

            def split_mm(dst, xt, w_hi, w_lo, w_is_lhs, xs, ws):
                n = 0
                for c in range(KC):
                    for part, wp in ((0, w_hi), (0, w_lo), (1, w_hi)):
                        xo, wo_ = xt[:, part, c, xs], wp[:, c, ws]
                        a, bb = (wo_, xo) if w_is_lhs else (xo, wo_)
                        ins = mm(dst, a, bb, start=(n == 0), stop=(n == 3 * KC - 1))
                        n += 1
                return ins

            def v_tiles(b):
                ln_done("attn", b)
                for tt in range(TT):
                    split_mm(tile_bank(V_BANK[0], tt), xt_a, wqkv_hi, wqkv_lo, False, slice(tt * P, (tt + 1) * P),
                             slice(2 * DIM, 3 * DIM)).then_inc(s["qkv_v"], 1)

            def qk_tile(b, tt):
                if tt >= 2:
                    pe.wait_ge(s["vev"], b * TT + 2 * (tt - 1))
                split_mm(ps[:, QKV_BANK[tt], :], xt_a, wqkv_hi, wqkv_lo, False, slice(tt * P, (tt + 1) * P),
                         slice(0, 2 * DIM)).then_inc(s["qkv"], 1)

            def qk_transposes(b):
                pe.wait_ge(s["qlo"], 2 * (b + 1))
                pe.wait_ge(s["shifts"], 2 * (b + 1))
                for j in range(8):
                    if j >= 4:
                        pe.wait_ge(s["qkta"] if j % 2 == 0 else s["qktv"], b * 4 + (j - 4) // 2 + 1)
                    q_or_k_transposes(j).then_inc(s["qktp"], 1)
                pe.wait_ge(s["qkta"], 4 * (b + 1))
                pe.wait_ge(s["qktv"], 4 * (b + 1))
                with pe.If(need_max == 1):
                    guard(b)
                with pe.Else():
                    pe.sem_inc(s["waited"], 1)

            def pre(b):
                ln_transposes("attn", b)
                v_tiles(b)
                for tt in range(TT):
                    qk_tile(b, tt)
                qk_transposes(b)

            def body(b, has_a, has_m, has_next):
                m = b - 1

                def scores(i):
                    h, k0 = unit(i)
                    r, hp = (h % 2) * ROWS, h // 2
                    if i >= 2:
                        pe.wait_ge(s["prob"], b * UNITS + i - 1)
                    for kk in range(2):
                        ins = mm(ps[:, 2 * (i % 2) + kk, :], kt[r:r + ROWS, hp, (k0 + kk) * P:(k0 + kk + 1) * P],
                                 qt[r:r + ROWS, hp, :], start=True, stop=True)
                    ins.then_inc(s["score"], 1)

                def values(k, kk):
                    g, pair = k // 2, k % 2
                    kc = 2 * pair + kk
                    if has_m and kc == 0 and g == 0:
                        pe.wait_ge(s["rescp"], b * DT)
                    if kc == 0 and g >= 1:
                        pe.wait_ge(s["on"], b * NG + g)
                    if kk == 0:
                        pe.wait_ge(s["prob"], b * UNITS + GROUP * (k + 1))
                    for j in range(GROUP):
                        ins = mm(ps[32 * j:32 * j + 32, 6, :], vaug[:, kc, g * GROUP + j, :],
                                 prob[:, (k * GROUP + j) % PSLOTS, kk, :], start=(kc == 0), stop=(kc == TT - 1))
                    if kk == 1:
                        ins.then_inc(s["pv"], 1)

                def out_rows(g):
                    pe.wait_ge(s["oev"], b * NG + g + 1)
                    for tt in range(TT):
                        ins = tp(ps[:, 6, tt * P:(tt + 1) * P], ot[:, tt * P:(tt + 1) * P], identf[:, :])
                    ins.then_inc(s["otp"], 1)

                def states(n, tiles):
                    if n == 0:
                        pe.wait_ge(s["delta"], b * DT)
                        pe.wait_ge(s["cev"], b)
                    pe.wait_ge(s["scan"], m * NS + n + 1)
                    for tt in tiles:
                        j = n * TT + tt
                        if j == 2:
                            pe.wait_ge(s["rescp"], b * DT)
                        if j >= 3:
                            pe.wait_ge(s["accd"], m * NS * TT + j - 2)
                        for d in range(DT):
                            ins = tp(ps[:, STATE_BANK[j % 3], d * P:(d + 1) * P], hst[:, n % HSLOTS, d, tt * P:(tt + 1) * P], identf[:, :])
                        ins.then_inc(s["htp"], 1)

                def y_transposes(tiles):
                    pe.wait_ge(s["accd"], b * NS * TT)
                    for d in tiles:
                        if d >= 3:
                            pe.wait_ge(s["yskip"], m * DT + d - 2)
                        for tt in range(TT):
                            ins = tp(ps[:, Y_BANK[d], tt * P:(tt + 1) * P], acc[:, tt, d * P:(d + 1) * P], identf[:, :])
                        ins.then_inc(s["ytp"], 1)

                def w_out(tt):
                    if tt == 0:
                        pe.wait_ge(s["y"], b * DT)
                    for d in range(DT):
                        ins = mm(tile_bank(2, tt), ybuf[:, d, tt * P:(tt + 1) * P], wout[:, d, :],
                                 start=(d == 0), stop=(d == DT - 1))
                    ins.then_inc(s["wo"], 1)

                for n in range(NS + 1 + LAG):
                    k = n - LAG
                    pv = None
                    if has_a and 0 <= k < NS and k % GROUP == GROUP - 1:
                        pv = 2 * (k // GROUP)
                    if has_a and k > 0 and k % GROUP == 0:
                        pv = 2 * (k // GROUP) - 1
                    if has_m and n == NS + 1:
                        y_transposes((0, 1))
                    if has_a and 0 <= k < NS:
                        scores(2 * k)
                    if has_m and n < NS:
                        states(n, (0, 1))
                    if has_m and n == NS + 1:
                        y_transposes((2, 3))
                    if has_a and 0 <= k < NS:
                        scores(2 * k + 1)
                    if pv is not None:
                        values(pv, 0)
                        values(pv, 1)
                    if has_m and n < NS:
                        states(n, (2, 3))
                    if has_a and k > GROUP and k % GROUP == 1:
                        out_rows(k // GROUP - 1)
                if has_m:
                    w_out(0)
                if has_a:
                    out_rows(NG - 1)
                if has_a:
                    pe.wait_ge(s["on"], (b + 1) * NG)
                    if has_m:
                        pe.wait_ge(s["yskip"], b * DT)
                    for c in range(KC):
                        for tt in range(TT):
                            ins = tp(ps[:, 4 + c, tt * P:(tt + 1) * P], on[:, tt, c * P:(c + 1) * P], identf[:, :])
                    ins.then_inc(s["ontp"], 1)
                if has_m:
                    w_out(1)
                if has_a:
                    pe.wait_ge(s["ocev"], b + 1)
                    for tt in range(TT):
                        for c in range(KC):
                            ins = mm(tile_bank(6, tt), oc[:, c, tt * P:(tt + 1) * P], wproj[:, c, :],
                                     start=(c == 0), stop=(c == KC - 1))
                        ins.then_inc(s["proj"], 1)
                if has_m:
                    w_out(2)
                    w_out(3)
                if has_a:
                    ln_transposes("ffn1", b)
                    qkv = {4: [lambda: ln_transposes("attn", b + 1)], 6: [lambda: v_tiles(b + 1)],
                           7: [lambda: qk_tile(b + 1, 0)], 8: [lambda: qk_tile(b + 1, 1)],
                           9: [lambda: qk_tile(b + 1, 2)]}
                    ffn(1, b, "ffn1", b, qkv if has_next else {})
                    if has_next:
                        qk_tile(b + 1, 3)
                if has_m:
                    if has_next:
                        pe.wait_ge(s["msq_sq"], (b + 1) * TT + 2)
                    ln_transposes("ffn2", b)
                if has_m and has_next:
                    pe.wait_ge(s["msq_sq"], (b + 2) * TT)
                every = slice(0, SEQ)

                def w_x():
                    ln_done("scan", b)
                    split_mm(ps[0:XD, WX_BANK, :], xt_b, wx_hi, wx_lo, True, every, slice(0, XD)).then_inc(s["xdp"], 1)

                def w_in_x(d):
                    if X_BANK[d] == WX_BANK:
                        pe.wait_ge(s["xdev"], b + 1)
                    split_mm(ps[:, X_BANK[d], :], xt_b, win_hi, win_lo, True, every,
                             slice(d * P, (d + 1) * P)).then_inc(s["xin"], 1)

                def w_in_res(d):
                    if d < 2:
                        pe.wait_ge(s["delta"], b * DT + d + 1)
                    else:
                        pe.wait_ge(s["rescp"], b * DT + d - 1)
                    split_mm(ps[:, RES_BANK[d], :], xt_b, win_hi, win_lo, True, every,
                             slice(D_INNER + d * P, D_INNER + (d + 1) * P)).then_inc(s["res"], 1)

                def c_rows():
                    pe.wait_ge(s["xcp"], b * DT + 1)
                    for tt in range(TT):
                        ins = tp(ps[:, C_BANK, tt * P:tt * P + XD], xdbl[:, tt * P:(tt + 1) * P], identf[0:XD, 0:XD])
                    ins.then_inc(s["ctp"], 1)

                def w_dt(d):
                    if d < DT - 1:
                        pe.wait_ge(s["xcp"], b * DT + d + 2)
                    else:
                        pe.wait_ge(s["cev"], b + 1)
                    mm(ps[:, DT_BANK[d], :], wdt[:, d * P:(d + 1) * P], xdbl[0:RANK, :], start=True,
                       stop=True).then_inc(s["dtp"], 1)

                scan_in = {2: [lambda: ln_transposes("scan", b)], 3: [w_x, lambda: w_in_x(0), lambda: w_in_x(1)],
                           4: [lambda: w_in_x(2), lambda: w_in_x(3)], 5: [c_rows, lambda: w_dt(0), lambda: w_dt(1)],
                           6: [lambda: w_dt(2), lambda: w_dt(3)], 9: [lambda: w_in_res(0), lambda: w_in_res(1)]}
                if has_m:
                    ffn(2, m, "ffn2", b, scan_in if has_a else {})
                else:
                    for steps in scan_in.values():
                        for step in steps:
                            step()
                    pe.sem_inc(s["down2"], 1)
                if has_a:
                    w_in_res(2)
                    w_in_res(3)
                if has_next:
                    if has_m:
                        pe.wait_ge(s["fout2"], b * TT)
                    qk_transposes(b + 1)
            iterations(pe, pre, body)


_INS = ['L0_attn_a_x', 'L0_attn_a_w_qkv', 'L0_attn_a_q_scale', 'L0_attn_a_k_scale', 'L0_attn_a_w_proj',
        'L0_attn_a_b_proj', 'L0_attn_b_W_in', 'L0_attn_b_K_conv', 'L0_attn_b_b_conv', 'L0_attn_b_W_x',
        'L0_attn_b_W_dt', 'L0_attn_b_b_dt', 'L0_attn_b_A_log', 'L0_attn_b_D', 'L0_attn_b_W_out',
        'L0_attn_b_b_out', 'L0_ffn_W1', 'L0_ffn_b1', 'L0_ffn_W2', 'L0_ffn_b2']


def rope_tables():
    import numpy as _np
    freqs = (1.0 / _np.float32(2500) ** (_np.arange(HALF, dtype=_np.float32) / HALF)).astype(_np.float32)
    angle = _np.outer(_np.arange(SEQ, dtype=_np.float32), freqs).astype(_np.float32).astype(_np.float64)
    cos, sin = _np.cos(angle), _np.sin(angle)
    return (_np.concatenate([cos, cos], 1).astype(_np.float32), _np.concatenate([-sin, sin], 1).astype(_np.float32))


def kernel(**inputs):
    import numpy as _np
    import concourse.bacc as _bacc
    from concourse.bass_utils import run_bass_kernel_spmd as _run

    nc = _bacc.Bacc("TRN2", target_bir_lowering=False, num_devices=1)
    arrays, aps = {}, {}
    for name in _INS:
        a = _np.ascontiguousarray(inputs[name])
        arrays["in_" + name] = a
        aps[name] = nc.dram_tensor("in_" + name, a.shape, mybir.dt.from_np(a.dtype), kind="ExternalInput").ap()
    tables = []
    for name, a in zip(("rope_cos", "rope_sin"), rope_tables()):
        arrays[name] = a
        tables.append(nc.dram_tensor(name, a.shape, mybir.dt.from_np(a.dtype), kind="ExternalInput").ap())
    bt = nc.dram_tensor("b_rows", (NS, SEQ), FP32, kind="Internal").ap()
    out = nc.dram_tensor("out_0", (BATCH, SEQ, DIM), FP32, kind="ExternalOutput").ap()
    hybrid_block(nc, aps, out, tables[0], tables[1], bt)
    r = _run(nc, [arrays], core_ids=[0])
    return r.results[0]["out_0"]
```
